# Optimizing a Trainium2 kernel written in Bass

```python
import numpy as np
import jax
import jax.numpy as jnp

def _softmax(x, axis=-1):
    return jax.nn.softmax(x, axis=axis)

def _gelu(x):
    return jax.nn.gelu(x, approximate=True)

def _silu(x):
    return jax.nn.silu(x)

def _sigmoid(x):
    return jax.nn.sigmoid(x)

def _layernorm(x, axis=-1, eps=1e-05):
    m = jnp.mean(x, axis=axis, keepdims=True)
    v = jnp.var(x, axis=axis, keepdims=True)
    return (x - m) / jnp.sqrt(v + eps)

def _scatter_add(tgt, idx, src, axis=0):
    return tgt.at[idx].add(src)

def _segment_sum(src, seg, n):
    return jax.ops.segment_sum(src, seg, n)
kernel_name = 'mk_gps_d1_gnn_r8_d37a01'

def setup_inputs(seed: int=0):
    np.random.seed(seed)
    _w = jnp.asarray

    def _rec_inputs():
        import jax
        import jax.numpy as jnp
        _gk = jax.random.key(seed)
        x = -0.0003713 + 1 * jax.random.normal(jax.random.fold_in(_gk, 1), (6250, 256), jnp.float32)
        src = jax.random.randint(jax.random.fold_in(_gk, 2), (100000,), 0, 6250, jnp.int32)
        dst = jnp.minimum((6250 * jax.random.uniform(jax.random.fold_in(_gk, 3), (100000,)) ** 2.0).astype(jnp.int32), 49999)
        _o = jnp.argsort(dst, stable=True)
        src = src[_o]
        dst = dst[_o]
        return (x, src, dst)
    x, src, dst = _rec_inputs()

    def _L0_gnn_setup():
        import jax, jax.numpy as jnp
        import numpy as np
        N = 6250
        E = 200000
        F_IN = 256
        F_OUT = 256
        ALPHA = 0.2
        key = jax.random.key(seed)
        ks = jax.random.split(key, 7)
        x = jax.random.normal(ks[0], (N, F_IN), dtype=jnp.float32)
        row = jax.random.randint(ks[1], (E,), 0, N, dtype=jnp.int32)
        col = jax.random.randint(ks[2], (E,), 0, N, dtype=jnp.int32)
        W_w = jax.random.normal(ks[3], (F_IN, F_OUT), dtype=jnp.float32) / np.sqrt(F_IN).astype(np.float32)
        W_b = jax.random.normal(ks[4], (F_OUT,), dtype=jnp.float32) * 0.01
        a_w = jax.random.normal(ks[5], (2 * F_OUT,), dtype=jnp.float32) / np.sqrt(2 * F_OUT).astype(np.float32)
        a_b = jax.random.normal(ks[6], (1,), dtype=jnp.float32) * 0.01
        return {'x': x, 'W_w': W_w, 'W_b': W_b, 'a_w': a_w, 'a_b': a_b, 'row': row, 'col': col}
    _L0_gnn_all = _L0_gnn_setup()
    _L0_gnn_in = {k: v for k, v in _L0_gnn_all.items() if k in ('W_w', 'W_b', 'a_w', 'a_b')}
    del _L0_gnn_all

    def _L0_mix_setup():
        import jax, jax.numpy as jnp
        import numpy as np
        NUM_HEADS = 8
        key = jax.random.key(seed)
        ks = jax.random.split(key, 5)
        B, N, C = (8, 2048, 256)
        x = jax.random.normal(ks[0], (B, N, C), dtype=jnp.float32)
        Wq = jax.random.normal(ks[1], (C, C), dtype=jnp.float32) * 0.02
        Wkv = jax.random.normal(ks[2], (2 * C, C), dtype=jnp.float32) * 0.02
        Wproj = jax.random.normal(ks[3], (C, C), dtype=jnp.float32) * 0.02
        bproj = jnp.zeros((C,), dtype=jnp.float32)
        return {'x': x, 'Wq': Wq, 'Wkv': Wkv, 'Wproj': Wproj, 'bproj': bproj}
    _L0_mix_all = _L0_mix_setup()
    _L0_mix_in = {k: v for k, v in _L0_mix_all.items() if k in ('Wq', 'Wkv', 'Wproj', 'bproj')}
    del _L0_mix_all

    def _L0_ffn_setup():
        import jax, jax.numpy as jnp
        import numpy as np
        NUM_EXPERTS = 8
        TOP_K = 2
        B, S, D = (8, 1024, 256)

        def _moe(tokens, router_w, w1, b1, w2, b2):
            N = tokens.shape[0]
            E = router_w.shape[0]
            logits = tokens.astype(jnp.float32) @ router_w.astype(jnp.float32).T
            probs = jax.nn.softmax(logits, axis=-1)
            rw, re = jax.lax.top_k(probs, TOP_K)
            if TOP_K > 1:
                rw = rw / jnp.maximum(rw.sum(-1, keepdims=True), 1e-12)
            rw = rw.astype(tokens.dtype)
            combine = jnp.zeros((N, E), tokens.dtype).at[jnp.arange(N)[:, None], re].set(rw)
            out = tokens
            for e in range(E):
                h = jax.nn.gelu(tokens @ w1[e] + b1[e], approximate=False)
                y = h @ w2[e] + b2[e]
                out = out + combine[:, e:e + 1] * y
            return out
        key = jax.random.key(seed)
        ks = jax.random.split(key, 4)
        scale = 1.0 / np.sqrt(D).astype(np.float32)
        return {'input_embeddings': jax.random.normal(ks[0], (B, S, D), jnp.float32), 'router_w': jax.random.normal(ks[1], (NUM_EXPERTS, D), jnp.float32) * scale, 'w1': jax.random.normal(ks[2], (NUM_EXPERTS, D, D), jnp.float32) * scale, 'b1': jnp.zeros((NUM_EXPERTS, D), jnp.float32), 'w2': jax.random.normal(ks[3], (NUM_EXPERTS, D, D), jnp.float32) * scale, 'b2': jnp.zeros((NUM_EXPERTS, D), jnp.float32)}
    _L0_ffn_all = _L0_ffn_setup()
    _L0_ffn_in = {k: v for k, v in _L0_ffn_all.items() if k in ('router_w', 'w1', 'b1', 'w2', 'b2')}
    del _L0_ffn_all
    return {'x': x, 'src': src, 'dst': dst, 'L0_gnn_W_w': _L0_gnn_in['W_w'], 'L0_gnn_W_b': _L0_gnn_in['W_b'], 'L0_gnn_a_w': _L0_gnn_in['a_w'], 'L0_gnn_a_b': _L0_gnn_in['a_b'], 'L0_mix_Wq': _L0_mix_in['Wq'], 'L0_mix_Wkv': _L0_mix_in['Wkv'], 'L0_mix_Wproj': _L0_mix_in['Wproj'], 'L0_mix_bproj': _L0_mix_in['bproj'], 'L0_ffn_router_w': _L0_ffn_in['router_w'], 'L0_ffn_w1': _L0_ffn_in['w1'], 'L0_ffn_b1': _L0_ffn_in['b1'], 'L0_ffn_w2': _L0_ffn_in['w2'], 'L0_ffn_b2': _L0_ffn_in['b2']}

def reference(x, src, dst, L0_gnn_W_w, L0_gnn_W_b, L0_gnn_a_w, L0_gnn_a_b, L0_mix_Wq, L0_mix_Wkv, L0_mix_Wproj, L0_mix_bproj, L0_ffn_router_w, L0_ffn_w1, L0_ffn_b1, L0_ffn_w2, L0_ffn_b2):
    import jax
    import jax.numpy as jnp

    def _L0_gnn_ref(x, W_w, W_b, a_w, a_b, row, col):
        import jax, jax.numpy as jnp
        import numpy as np
        N = 6250
        E = 200000
        F_IN = 256
        F_OUT = 256
        ALPHA = 0.2
        Wh = x @ W_w + W_b
        f_dst_part = Wh @ a_w[:F_OUT]
        f_row_part = Wh @ a_w[F_OUT:]
        e = f_dst_part[col] + f_row_part[row] + a_b[0]
        e = jnp.where(e > 0, e, ALPHA * e)
        m = jax.ops.segment_max(e, row, num_segments=N)
        ex = jnp.exp(e - m[row])
        denom = jax.ops.segment_sum(ex, row, num_segments=N)
        att = ex / denom[row]
        h_prime = jax.ops.segment_sum(att[:, None] * Wh[col], row, num_segments=N)
        return jax.nn.relu(h_prime)

    def _L0_mix_ref(x, Wq, Wkv, Wproj, bproj):
        import jax, jax.numpy as jnp
        import numpy as np
        NUM_HEADS = 8
        B, N, C = x.shape
        h = NUM_HEADS
        d = C // h
        q = jnp.einsum('bnc,oc->bno', x, Wq).reshape(B, N, h, d).transpose(0, 2, 1, 3)
        kv = jnp.einsum('bnc,oc->bno', x, Wkv).reshape(B, N, 2, h, d)
        k = kv[:, :, 0].transpose(0, 2, 1, 3)
        v = kv[:, :, 1].transpose(0, 2, 1, 3)
        q = jax.nn.elu(q) + 1.0
        k = jax.nn.elu(k) + 1.0
        k_sum = k.sum(axis=2)
        D_inv = 1.0 / jnp.maximum(jnp.einsum('bhnd,bhd->bhn', q, k_sum), 1e-06)
        context = jnp.einsum('bhnd,bhne->bhde', k, v)
        attn = jnp.einsum('bhnd,bhde->bhne', q, context) * D_inv[..., None]
        out = attn.transpose(0, 2, 1, 3).reshape(B, N, C)
        out = jnp.einsum('bnc,oc->bno', out, Wproj) + bproj
        return out

    def _L0_ffn_ref(input_embeddings, router_w, w1, b1, w2, b2):
        import jax, jax.numpy as jnp
        import numpy as np
        NUM_EXPERTS = 8
        TOP_K = 2
        B, S, D = (8, 1024, 256)

        def _moe(tokens, router_w, w1, b1, w2, b2):
            N = tokens.shape[0]
            E = router_w.shape[0]
            logits = tokens.astype(jnp.float32) @ router_w.astype(jnp.float32).T
            probs = jax.nn.softmax(logits, axis=-1)
            rw, re = jax.lax.top_k(probs, TOP_K)
            if TOP_K > 1:
                rw = rw / jnp.maximum(rw.sum(-1, keepdims=True), 1e-12)
            rw = rw.astype(tokens.dtype)
            combine = jnp.zeros((N, E), tokens.dtype).at[jnp.arange(N)[:, None], re].set(rw)
            out = tokens
            for e in range(E):
                h = jax.nn.gelu(tokens @ w1[e] + b1[e], approximate=False)
                y = h @ w2[e] + b2[e]
                out = out + combine[:, e:e + 1] * y
            return out
        b, s, d = input_embeddings.shape
        tokens = input_embeddings.reshape(b * s, d)
        return _moe(tokens, router_w, w1, b1, w2, b2).reshape(b, s, d)
    xn = _layernorm(x, axis=-1)
    x = x + _L0_gnn_ref(xn, L0_gnn_W_w, L0_gnn_W_b, L0_gnn_a_w, L0_gnn_a_b, src, dst) + _L0_mix_ref(xn[None], L0_mix_Wq, L0_mix_Wkv, L0_mix_Wproj, L0_mix_bproj)[0]
    x = x + _L0_ffn_ref(_layernorm(x, axis=-1)[None], L0_ffn_router_w, L0_ffn_w1, L0_ffn_b1, L0_ffn_w2, L0_ffn_b2)[0]
    return x

_drawn_inputs = setup_inputs


def setup_inputs(seed=0):
    import zlib

    import numpy as np

    out = dict(_drawn_inputs(seed))
    spreads = {'L0_mix_bproj': (0.0, 0.1), 'L0_ffn_b1': (0.0, 0.327), 'L0_ffn_b2': (0.0, 0.1)}
    factors = {'L0_gnn_W_b': 3.9, 'L0_mix_Wq': 8.0, 'L0_mix_Wkv': 8.0, 'L0_mix_Wproj': 8.0}
    for name, (base, spread) in spreads.items():
        noise = np.random.default_rng([zlib.crc32(name.encode()), seed]).standard_normal(out[name].shape)
        drawn = base * np.exp(spread * noise) if base else spread * noise
        out[name] = jnp.asarray(drawn.astype(out[name].dtype))
    for name, factor in factors.items():
        out[name] = (out[name] * factor).astype(out[name].dtype)
    return out
```

```python
from contextlib import ExitStack

import concourse.bass as bass
from concourse import mybir

F32 = mybir.dt.float32
I32 = mybir.dt.int32
U16 = mybir.dt.uint16
BF16 = mybir.dt.bfloat16
ALU = mybir.AluOpType
ACT = mybir.ActivationFunctionType
AX = mybir.AxisListType

P = 128
ds = bass.ds


def graph_layer(nc, x, src, dst, W_w, W_b, a_w, a_b, Wq, Wkv, Wproj, bproj, router_w, w1, b1, w2, b2, out):
    N, D = x.shape
    E = src.shape[0]
    X = router_w.shape[0]
    H = 8
    DH = D // H
    ALPHA = 0.2
    W = -(-N // P)
    LAST = N - (W - 1) * P
    EC = -(-E // P)
    EFULL = E // EC
    EREST = E - EFULL * EC
    GT = 4
    T = E // P + W
    T = -(-T // (4 * GT)) * 4 * GT
    TP = T + -(-EC // P) + 1
    NG = T // GT
    GR = 4
    SC = 16
    SH = SC // 2
    TW = D + 2
    TM = T + GT

    table = nc.dram_tensor("table", [W * P, TW], F32).ap()
    binned = nc.dram_tensor("binned", [P * TP, 2], I32).ap()

    with ExitStack() as ctx:
        def sb(name, shape, dt=F32):
            return ctx.enter_context(nc.sbuf_tensor(name, shape, dt))

        def sem(name):
            return ctx.enter_context(nc.semaphore(name))

        xs = sb("xs", [P, W, D])
        work = sb("work", [P, W * TW])
        tab = work[:, :].rearrange("p (w c) -> p w c", w=W)
        place = [0]

        def part(*shape):
            n = 1
            for k in shape:
                n *= k
            a, place[0] = place[0], place[0] + n
            assert place[0] <= W * TW
            names = [f"d{k}" for k in range(len(shape))]
            v = work[:, a:a + n]
            if len(shape) > 1:
                v = v.rearrange(f"p ({' '.join(names)}) -> p {' '.join(names)}", **dict(zip(names, shape)))
            return v

        big = sb("big", [P, 2 * W * P])
        qT = big[:, :].rearrange("p (h n) -> p h n", h=2)
        w1s = big[:, 0:X * 2 * D].rearrange("p (e h f) -> p e h f", e=X, h=2)
        w2s = big[:, X * 2 * D:X * 4 * D].rearrange("p (e h f) -> p e h f", e=X, h=2)
        wraw = big[:, 0:8 * D].rearrange("p (n c) -> p n c", n=8)
        b1r = big[0:X, 8 * D:9 * D]
        rws = big[0:X, 9 * D:10 * D]
        b1c = sb("b1c", [P, 2, X])
        b2s = sb("b2s", [X, D])
        rwT = sb("rwT", [P, 2, X])
        wws = sb("wws", [P, 2, D])
        wkvT = sb("wkvT", [P, 2, 2 * D])
        wqT = sb("wqT", [P, 2, D])
        wpT = sb("wpT", [P, 2, D])
        wbb = sb("wbb", [P, D])
        adst = sb("adst", [P, D])
        asrc = sb("asrc", [P, D])
        abb = sb("abb", [P, 1])
        bpb = sb("bpb", [P, D])
        ident = sb("ident", [P, P])
        onesf = sb("onesf", [P, P])
        before = sb("before", [P, P])
        iotap = sb("iotap", [P, P])
        valid = sb("valid", [P, W])
        epsc = sb("epsc", [P, 1])
        srci = part(EC).bitcast(I32)
        dsti = part(EC).bitcast(I32)
        rank = part(EC)
        posf = part(EC)
        winb = part(EC // 2).bitcast(BF16)
        maskb = part(EC // 2).bitcast(BF16)
        onebf = part(EC // 2).bitcast(BF16)
        slot = sb("slot", [P, EC], I32)
        lst = sb("lst", [P, TP, 2], I32)
        rec = lst[:, 0:EC, :]
        cnt = sb("cnt", [P, W])
        ntf = sb("ntf", [P, W])
        nti = sb("nti", [P, W], I32)
        tend = sb("tend", [P, W])
        tendi = sb("tendi", [P, W + 1], I32)
        base = sb("base", [P, W])
        ntc = sb("ntc", [64, 1])
        ntci = sb("ntci", [64, 1], I32)
        tec = sb("tec", [64, 1])
        tsc = sb("tsc", [64, 1])
        sidx = sb("sidx", [P, 2, SH], I32)
        srec = sb("srec", [P, 2, SH, 2], I32)
        stats = sb("stats", [P, 6])
        agg = sb("agg", [P, 2])
        idle = sb("idle", [P, 1])
        rest = sb("rest", [P, 1])
        mv = sb("mv", [P, W, 2])
        sd = sb("sd", [P, W])
        rs = sb("rs", [P, W])
        xn = sb("xn", [P, D])
        xnT = sb("xnT", [P, 2, P])
        frc = sb("frc", [P, W])
        ek = sb("ek", [P, D])
        rk = sb("rk", [P, D])
        kk = sb("kk", [P, D])
        vv = sb("vv", [P, D + 1])
        eq = sb("eq", [P, D])
        rq = sb("rq", [P, D])
        cmax = sb("cmax", [P, 1])
        c1 = sb("c1", [1, 1])
        coff = sb("coff", [P, 1])
        frT = sb("frT", [64, P])
        inw = sb("inw", [64, TM])
        stw = sb("stw", [64, TM])
        meta = sb("meta", [P, TM, 3])
        bd = sb("bd", [P, 2, D + H])
        dinv = sb("dinv", [P, H])
        dmx = sb("dmx", [P, H])
        gidx = sb("gidx", [P, GR, GT], I32)
        place[0] = 0
        G = part(GR, GT, TW)
        V = part(2, GT, P)
        OT = part(2, GT, P)
        S = part(2, GT, P)
        qs = part(2, P)
        att = part(D)
        attT = part(2, P)
        mixs = part(D)
        U = part(D + 1)
        hh = part(D)
        x2 = part(D)
        x2T = part(2, P)
        acc = part(D)
        hT = part(2, 2, P)
        m4 = sb("m4", [P, 2, GT, 3])
        fdp = sb("fdp", [P, 2, GT])
        mloc = sb("mloc", [P, 2, GT])
        mx = sb("mx", [P, 2, GT])
        cc = sb("cc", [P, 2, GT])
        pr = sb("pr", [P, 2, GT, 2])
        gd = sb("gd", [P, 2, GT])
        gc = sb("gc", [P, 2, GT])
        ge = sb("ge", [P, 2, GT])
        gg = sb("gg", [P, 2, GT])
        s1 = sb("s1", [P, 2, GT])
        s2 = sb("s2", [P, 2, GT])
        s3 = sb("s3", [P, 2, GT])
        s4 = sb("s4", [P, 2, GT])
        w4 = sb("w4", [P, 2, GT])
        dn = sb("dn", [P, 1])
        rd = sb("rd", [P, 1])
        lg = sb("lg", [P, X])
        mx8 = sb("mx8", [P, 8])
        ix8 = sb("ix8", [P, 8], mybir.dt.uint32)
        ixf = sb("ixf", [P, 8])
        nm = sb("nm", [P, 1])
        ex = sb("ex", [P, X])
        e8 = sb("e8", [P, 8])
        sm = sb("sm", [P, 1])
        rsm = sb("rsm", [P, 1])
        p8 = sb("p8", [P, 8])
        tot = sb("tot", [P, 1])
        totc = sb("totc", [P, 1])
        rt = sb("rt", [P, 1])
        ww = sb("ww", [P, 2])
        cA = sb("cA", [P, X])
        cB = sb("cB", [P, X])
        comb = sb("comb", [P, X])
        combT = sb("combT", [X, P])

        bank = [ctx.enter_context(nc.psum_tensor(f"bank{n}", [P, 512], F32)) for n in range(8)]

        loaded = {n: sem("loaded_" + n) for n in ("edges", "x", "raw", "weights", "experts", "list")}
        filled = sem("filled")
        consts = sem("consts")
        masks = sem("masks")
        blank = sem("blank")
        dv = sem("dv")
        counted, ranked = sem("counted"), sem("ranked")
        prefix, ntc_done, slot_done = sem("prefix"), sem("ntc_done"), sem("slot_done")
        staged = [sem(f"staged{i}") for i in range(2)]
        scattered = [sem(f"scattered{i}") for i in range(2)]
        wt_ps, wt_sb = sem("wt_ps"), sem("wt_sb")
        stat1, stat2, stat3, std_done, rstd_done = sem("stat1"), sem("stat2"), sem("stat3"), sem("std_done"), sem("rstd_done")
        n_xn, n_xt, n_xnT, n_wh, n_kv, n_q, n_tab, n_tab2, n_fd, n_kraw, n_kk, n_qraw, n_qT, n_ctx = (
            sem("n_" + k) for k in ("xn", "xt", "xnT", "wh", "kv", "q", "tab", "tab2", "fd", "kraw", "kk", "qraw", "qT",
                                    "ctx"))
        ctx_zero = sem("ctx_zero")
        table_out = sem("table_out")
        c_in, c_ps = sem("c_in"), sem("c_ps")
        tiles_in, meta_ps, meta_sb = sem("tiles_in"), sem("meta_ps"), sem("meta_sb")
        bd_done = sem("bd_done")
        a_qs, a_num, a_dm, a_di, a_att, a_at, a_attT, a_pj, a_mix, a_x = (
            sem("a_" + k) for k in ("qs", "num", "dm", "di", "att", "at", "attT", "pj", "mix", "x"))
        listed = [sem(f"listed{i}") for i in range(GR)]
        rows_in = [sem(f"rows_in{i}") for i in range(GR)]
        (e_m4, e_pr, e_fdp, e_V, e_VT, e_ml, e_mx, e_cc, e_R, e_gd, e_gc, e_ge, e_gg, e_OT, e_EX, e_s1, e_s2,
         e_s3, e_s4, e_w4, e_S, e_A, e_U) = (sem("e_" + k) for k in (
             "m4", "pr", "fdp", "V", "VT", "ml", "mx", "cc", "R", "gd", "gc", "ge", "gg", "OT", "EX", "s1", "s2",
             "s3", "s4", "w4", "S", "A", "U"))
        f_dn, f_rd, f_hh, f_x = (sem("f_" + k) for k in ("dn", "rd", "hh", "x"))
        (m_st, m_ag0, m_ag, m_sd, m_rs, m_x2, m_xt, m_xtc, m_lg, m_lgc, m_mx, m_ix, m_nm, m_ex, m_small, m_comb, m_ct,
         m_ctc, m_h, m_gl, m_y, m_acc0, m_acc, m_res, m_out) = (sem("m_" + k) for k in (
             "st", "ag0", "ag", "sd", "rs", "x2", "xt", "xtc", "lg", "lgc", "mx", "ix", "nm", "ex", "small", "comb", "ct",
             "ctc", "h", "gl", "y", "acc0", "acc", "res", "out"))

        binned_p = binned.rearrange("(p t) c -> p t c", t=TP)
        cuts = [(a, min(a + 512, TM)) for a in range(0, TM, 512)]

        def row(a, n):
            return a.rearrange("(a n) -> a n", a=1).to_broadcast([n, a.shape[0]])

        block = ctx.enter_context(nc.Block())

        @block.sync
        def _(sp):
            sp.wait_ge(filled, 2)
            a = EFULL // 16 * 16
            for arr, buf in ((src, srci), (dst, dsti)):
                sp.dma_start(buf[0:a, :], arr[0:a * EC].rearrange("(p c) -> p c", c=EC)).then_inc(loaded["edges"], 16)
                sp.dma_start(buf[a:EFULL, :], arr[a * EC:EFULL * EC].rearrange("(p c) -> p c", c=EC)
                             ).then_inc(loaded["edges"], 16)
                sp.dma_start(buf[EFULL:EFULL + 1, 0:EREST], arr[EFULL * EC:E].rearrange("(p c) -> p c", p=1)
                             ).then_inc(loaded["edges"], 16)
            sp.wait_ge(filled, 3)
            sp.dma_start(xs[:, 0:W - 1, :], x[0:(W - 1) * P, :].rearrange("(w p) c -> p w c", p=P)
                         ).then_inc(loaded["x"], 16)
            sp.dma_start(xs[0:LAST, W - 1, :], x[(W - 1) * P:N, :]).then_inc(loaded["x"], 16)
            sp.wait_ge(filled, 5)
            sp.dma_start(binned_p, lst[:, :, :]).then_inc(blank, 16)
            sp.dma_start(wraw[:, 0:2, :], Wq.rearrange("(h p) c -> p h c", p=P)).then_inc(loaded["raw"], 16)
            sp.dma_start(wraw[:, 2:6, :], Wkv.rearrange("(h p) c -> p h c", p=P)).then_inc(loaded["raw"], 16)
            sp.dma_start(wraw[:, 6:8, :], Wproj.rearrange("(h p) c -> p h c", p=P)).then_inc(loaded["raw"], 16)
            sp.dma_start(rws, router_w).then_inc(loaded["raw"], 16)
            sp.dma_start(b1r, b1).then_inc(loaded["raw"], 16)
            sp.dma_start(wws[:, :, :], W_w.rearrange("(h p) c -> p h c", p=P)).then_inc(loaded["weights"], 16)
            sp.dma_start(wbb[:, :], row(W_b, P)).then_inc(loaded["weights"], 16)
            sp.dma_start(adst[:, :], row(a_w[0:D], P)).then_inc(loaded["weights"], 16)
            sp.dma_start(asrc[:, :], row(a_w[D:2 * D], P)).then_inc(loaded["weights"], 16)
            sp.dma_start(abb[:, :], row(a_b, P)).then_inc(loaded["weights"], 16)
            sp.dma_start(bpb[:, :], row(bproj, P)).then_inc(loaded["weights"], 16)
            sp.dma_start(b2s[:, :], b2).then_inc(loaded["weights"], 16)
            sp.wait_ge(n_fd, 2 * W)
            sp.dma_start(table.rearrange("(w p) c -> p w c", p=P), tab[:, :, :]).then_inc(table_out, 16)
            sp.wait_ge(a_qs, W)
            sp.dma_start(w1s, w1.rearrange("e (h p) f -> p e h f", p=P)).then_inc(loaded["experts"], 16)
            sp.dma_start(w2s, w2.rearrange("e (h p) f -> p e h f", p=P)).then_inc(loaded["experts"], 16)
            sp.wait_ge(scattered[0], 16 * (SH * (EC // SC) + min(SH, EC % SC)))
            sp.wait_ge(scattered[1], 16 * (SH * (EC // SC) + max(0, EC % SC - SH)))
            sp.dma_start(lst[:, :, :], binned_p).then_inc(loaded["list"], 16)
            with sp.Fori(0, W - 1) as i:
                sp.wait_ge(m_res, i + 1)
                sp.dma_start(out[ds(i * P, P), :], xs[:, ds(i, 1), :].rearrange("p a c -> p (a c)")
                             ).then_inc(m_out, 16)
            sp.wait_ge(m_res, W)
            sp.dma_start(out[(W - 1) * P:N, :], xs[0:LAST, W - 1, :]).then_inc(m_out, 16)
            sp.wait_ge(m_out, 16 * W)

        @block.gpsimd
        def _(pool):
            pool.memset(srci, (W + 1) * P).then_inc(filled, 1)
            pool.memset(dsti, 0).then_inc(filled, 1)
            pool.memset(xs[:, W - 1, :], 0.0).then_inc(filled, 1)
            pool.memset(lst[:, :, 0], 0).then_inc(filled, 1)
            pool.memset(lst[:, :, 1], -1).then_inc(filled, 1)
            pool.iota(posf, pattern=[[1, EC]], base=T * P, channel_multiplier=0,
                      allow_small_or_imprecise_dtypes=True).then_inc(consts, 1)
            pool.iota(iotap[:, :], pattern=[[1, P]], base=0, channel_multiplier=0,
                      allow_small_or_imprecise_dtypes=True).then_inc(consts, 1)
            pool.memset(onesf[:, :], 1.0).then_inc(consts, 1)
            pool.memset(onebf, 1.0).then_inc(consts, 1)
            pool.memset(before[:, :], 1.0).then_inc(masks, 1)
            pool.memset(ident[:, :], 0.0).then_inc(masks, 1)
            pool.memset(valid[:, :], 1.0).then_inc(masks, 1)
            pool.wait_ge(masks, 3)
            pool.affine_select(out=before[:, :], in_=before[:, :], compare_op=ALU.is_gt, fill=0.0, base=0,
                               pattern=[[1, P]], channel_multiplier=-1).then_inc(consts, 1)
            pool.affine_select(out=ident[:, :], in_=ident[:, :], compare_op=ALU.not_equal, fill=1.0, base=0,
                               pattern=[[-1, P]], channel_multiplier=1).then_inc(consts, 1)
            pool.affine_select(out=valid[:, W - 1:W], in_=valid[:, W - 1:W], compare_op=ALU.is_gt, fill=0.0,
                               base=LAST, pattern=[[0, 1]], channel_multiplier=-1).then_inc(consts, 1)
            pool.memset(kk[:, 0:P], 0.0).then_inc(consts, 1)
            pool.memset(epsc[:, :], 1e-5).then_inc(consts, 1)
            pool.iota(inw[:, :], pattern=[[1, TM]], base=0, channel_multiplier=0,
                      allow_small_or_imprecise_dtypes=True).then_inc(consts, 1)

            pool.wait_ge(slot_done, 1)
            pool.wait_ge(blank, 16)

            def stage(c, n, b):
                pool.tensor_copy(sidx[:, b, 0:n], slot[:, c]).then_inc(staged[b], 1)
                pool.tensor_copy(srec[:, b, 0:n, :], rec[:, c, :]).then_inc(staged[b], 1)

            def scatter(b, n):
                pool.tensor_tensor(rest[:, :], iotap[:, 0:1], iotap[:, 0:1], ALU.add)
                for j in range(n):
                    pool.indirect_dma_start(binned, bass.IndirectOffsetOnAxis(ap=sidx[:, b, j:j + 1], axis=0),
                                            srec[:, b, j, :], None).then_inc(scattered[b], 16)

            for b in range(2):
                stage(slice(b * SH, (b + 1) * SH), SH, b)
                pool.wait_ge(staged[b], 2)
                scatter(b, SH)
            full = EC // SC
            with pool.Fori(1, full) as i:
                for b in range(2):
                    pool.wait_ge(scattered[b], i * (16 * SH))
                    stage(ds(i * SC + b * SH, SH), SH, b)
                    pool.wait_ge(staged[b], i * 2 + 2)
                    scatter(b, SH)
            for b in range(2):
                n = min(SH, EC - full * SC - b * SH)
                if n > 0:
                    pool.wait_ge(scattered[b], full * 16 * SH)
                    stage(slice(full * SC + b * SH, full * SC + b * SH + n), n, b)
                    pool.wait_ge(staged[b], full * 2 + 2)
                    scatter(b, n)

            pool.wait_ge(loaded["list"], 16)
            pool.wait_ge(table_out, 16)
            pool.wait_ge(c_in, 1)

            def gather(r, c, k):
                pool.tensor_copy(gidx[:, r, :], lst[:, c, 0]).then_inc(listed[r], 1)
                pool.wait_ge(listed[r], k)
                pool.tensor_tensor(rest[:, :], iotap[:, 0:1], iotap[:, 0:1], ALU.add)
                for j in range(GT):
                    pool.indirect_dma_start(G[:, r, j, :], None, table,
                                            bass.IndirectOffsetOnAxis(ap=gidx[:, r, j:j + 1], axis=0)
                                            ).then_inc(rows_in[r], 16)

            pool.wait_ge(a_x, W)
            for r in range(GR):
                gather(r, slice(r * GT, (r + 1) * GT), 1)
            with pool.Fori(1, NG // GR) as i:
                for r in range(GR):
                    pool.wait_ge(e_A, i * (GR * GT) + (r + 1 - GR) * GT)
                    gather(r, ds(i * (GR * GT) + r * GT, GT), i + 1)
            pool.wait_ge(e_A, (NG + 1 - GR) * GT)
            gather(0, slice(T, T + GT), NG // GR + 1)
            pool.wait_ge(rows_in[0], 16 * GT * (NG // GR + 1))

        @block.scalar
        def _(act):
            for n, o in enumerate((wqT[:, :, 0:P], wqT[:, :, P:D], wkvT[:, :, 0:P], wkvT[:, :, P:2 * P],
                                   wkvT[:, :, 2 * P:3 * P], wkvT[:, :, 3 * P:4 * P], wpT[:, :, 0:P],
                                   wpT[:, :, P:D])):
                act.wait_ge(wt_ps, n + 1)
                act.copy(o, bank[n][:, 0:D].rearrange("p (h c) -> p h c", h=2)).then_inc(wt_sb, 1)
            act.wait_ge(wt_ps, 9)
            act.copy(rwT[:, :, :], bank[0][:, 0:2 * X].rearrange("p (h c) -> p h c", h=2)).then_inc(wt_sb, 1)
            act.copy(b1c[:, :, :], bank[0][:, 2 * X:4 * X].rearrange("p (h e) -> p h e", h=2)).then_inc(wt_sb, 1)
            act.wait_ge(consts, 10)
            act.wait_ge(stat2, W)
            act.activation(sd[:, :], mv[:, :, 1], ACT.Sqrt, bias=epsc[:, :]).then_inc(std_done, 1)

            with act.Fori(0, W) as i:
                act.wait_ge(n_xt, i + 1)
                act.copy(xnT[:, :, :], bank[0][:, 0:D].rearrange("p (h c) -> p h c", h=2)).then_inc(n_xnT, 1)
                act.wait_ge(n_kv, i + 1)
                act.activation(ek[:, :], bank[2][:, 0:D], ACT.Exp)
                act.activation(rk[:, :], bank[2][:, 0:D], ACT.Relu)
                act.copy(vv[:, 0:D], bank[2][:, D:2 * D])
                act.copy(vv[:, D:D + 1], valid[:, ds(i, 1)]).then_inc(n_kraw, 1)
                act.wait_ge(n_q, i + 1)
                act.activation(eq[:, :], bank[3][:, 0:D], ACT.Exp)
                act.activation(rq[:, :], bank[3][:, 0:D], ACT.Relu).then_inc(n_qraw, 1)

            for n, (t0, t1) in enumerate(cuts):
                act.wait_ge(meta_ps, n + 1)
                act.activation(meta[:, t0:t1, 0], bank[2 * n][:, 0:t1 - t0], ACT.Identity, bias=abb[:, :])
                act.activation(meta[:, t0:t1, 1], bank[2 * n + 1][:, 0:t1 - t0], ACT.Copy, bias=1.0, scale=-1.0
                               ).then_inc(meta_sb, 1)

            act.wait_ge(table_out, 16)
            act.wait_ge(bd_done, 1)
            with act.Fori(0, W) as i:
                act.copy(qs[:, :, :], qT[:, :, ds(i * P, P)]).then_inc(a_qs, 1)
                act.wait_ge(a_at, i + 1)
                act.copy(attT[:, :, :], bank[6][:, 0:D].rearrange("p (h c) -> p h c", h=2)).then_inc(a_attT, 1)
                act.wait_ge(a_pj, i + 1)

            act.wait_ge(loaded["list"], 16)
            act.copy(meta[:, :, 2], lst[:, 0:TM, 1]).then_inc(meta_sb, 1)
            act.wait_ge(meta_sb, len(cuts) + 1)

            def front(g, b, c):
                act.copy(m4[:, b, :, :], meta[:, c, :]).then_inc(e_m4, 1)
                act.wait_ge(e_m4, g + 1)
                act.copy(pr[:, b, :, 0], m4[:, b, :, 0]).then_inc(e_pr, 1)
                act.wait_ge(e_ml, g + 1)
                act.activation(OT[:, b, :, :], bank[0][:, :].rearrange("p (j e) -> p j e", j=GT), ACT.Sign
                               ).then_inc(e_OT, 1)
                act.wait_ge(e_gc, g + 1)
                act.activation(ge[:, b, :], gc[:, b, :], ACT.Exp).then_inc(e_ge, 1)
                act.wait_ge(e_s4, g + 1)
                act.activation(w4[:, b, :], s4[:, b, :], ACT.Exp).then_inc(e_w4, 1)

            for g in range(2):
                front(g, g, slice(g * GT, (g + 1) * GT))
            with act.Fori(1, NG // 2) as i:
                for b in range(2):
                    act.wait_ge(e_S, i * 2 + (b - 1))
                    front(i * 2 + b, b, ds(i * (2 * GT) + b * GT, GT))
            act.wait_ge(e_S, NG - 1)
            front(NG, 0, slice(T, T + GT))

            act.wait_ge(m_ag, W)
            act.activation(sd[:, :], mv[:, :, 1], ACT.Sqrt, bias=epsc[:, :]).then_inc(m_sd, 1)
            with act.Fori(0, W) as i:
                act.wait_ge(m_xt, i + 1)
                act.copy(x2T[:, :, :], bank[0][:, 0:D].rearrange("p (h c) -> p h c", h=2)).then_inc(m_xtc, 1)
                act.wait_ge(m_nm, i + 1)
                act.activation(ex[:, :], lg[:, :], ACT.Exp, bias=nm[:, :], accum_out=sm[:, :])
                act.activation(e8[:, :], mx8[:, :], ACT.Exp, bias=nm[:, :]).then_inc(m_ex, 1)
                act.wait_ge(m_ct, i + 1)
                act.copy(combT[:, :], bank[2][0:X, 0:P]).then_inc(m_ctc, 1)
                for e in range(X):
                    act.wait_ge(m_h, i * X + (e + 1))
                    if e >= 2:
                        act.wait_ge(m_y, i * (X + 1) + (e - 1))
                    for f in range(2):
                        act.activation(hT[:, e % 2, f, :], bank[4 + e % 2][:, f * P:(f + 1) * P], ACT.Gelu,
                                       bias=b1c[:, f, e:e + 1]).then_inc(m_gl, 1)

        @block.tensor
        def _(pe):
            pe.wait_ge(consts, 10)
            pe.wait_ge(loaded["raw"], 16 * 5)
            for n in range(8):
                for h in range(2):
                    mm = pe.transpose(bank[n][:, h * P:(h + 1) * P], wraw[:, n, h * P:(h + 1) * P], ident[:, :])
                mm.then_inc(wt_ps, 1)
            pe.wait_ge(wt_sb, 1)
            for h in range(2):
                pe.transpose(bank[0][:, h * X:(h + 1) * X], rws[:, h * P:(h + 1) * P], ident[0:X, 0:X])
                mm = pe.transpose(bank[0][:, (2 + h) * X:(3 + h) * X], b1r[:, h * P:(h + 1) * P], ident[0:X, 0:X])
            mm.then_inc(wt_ps, 1)
            pe.wait_ge(wt_sb, 10)
            pe.wait_ge(counted, W)
            pe.matmul(bank[7][:, 0:W], before[:, :], cnt[:, :], start=True, stop=True)
            pe.matmul(bank[7][:, 64:64 + W], onesf[:, :], cnt[:, :], start=True, stop=True)
            pe.matmul(bank[7][0:W, 128:129], cnt[:, :], onesf[:, 0:1], start=True, stop=True).then_inc(prefix, 1)
            pe.wait_ge(ntc_done, 1)
            pe.matmul(bank[6][0:W, 0:1], before[0:W, 0:W], ntc[0:W, :], start=True, stop=True).then_inc(prefix, 1)

            pe.wait_ge(loaded["weights"], 16 * 7)
            for h in range(2):
                pe.matmul(bank[4 + h][:, 0:D + 1], kk[:, 0:P], wkvT[:, 0, 0:D + 1], start=True, stop=True)
            with pe.Fori(0, W) as i:
                pe.wait_ge(n_xn, i + 1)
                for h in range(2):
                    mm = pe.transpose(bank[0][:, h * P:(h + 1) * P], xn[:, h * P:(h + 1) * P], ident[:, :])
                mm.then_inc(n_xt, 1)
                pe.wait_ge(n_xnT, i + 1)
                for h in range(2):
                    mm = pe.matmul(bank[1][:, 0:D], xnT[:, h, :], wws[:, h, :], start=(h == 0), stop=(h == 1))
                mm.then_inc(n_wh, 1)
                for h in range(2):
                    mm = pe.matmul(bank[2][:, :], xnT[:, h, :], wkvT[:, h, :], start=(h == 0), stop=(h == 1))
                mm.then_inc(n_kv, 1)
                for o in range(2):
                    for h in range(2):
                        mm = pe.matmul(bank[3][:, o * P:(o + 1) * P], wqT[:, h, o * P:(o + 1) * P], xnT[:, h, :],
                                       start=(h == 0), stop=(h == 1))
                mm.then_inc(n_q, 1)
                pe.wait_ge(n_kk, i + 1)
                pe.wait_ge(n_qT, i + 1)
                for h in range(2):
                    mm = pe.matmul(bank[4 + h][:, 0:D + 1], kk[:, h * P:(h + 1) * P], vv[:, :], start=False,
                                   stop=True, skip_group_check=True)
                mm.then_inc(n_ctx, 1)

            pe.wait_ge(c_in, 1)
            pe.transpose(bank[6][0:1, 0:P], cmax[:, :], ident[:, :]).then_inc(c_ps, 1)
            pe.wait_ge(c_in, 2)
            pe.matmul(bank[6][:, 0:1], onesf[0:1, :], c1[:, :], start=True, stop=True).then_inc(c_ps, 1)
            pe.transpose(bank[7][0:W, 0:P], frc[:, :], ident[:, :]).then_inc(c_ps, 1)
            pe.wait_ge(tiles_in, 1)
            for n, (t0, t1) in enumerate(cuts):
                pe.matmul(bank[2 * n][:, 0:t1 - t0], frT[0:W, :], inw[0:W, t0:t1], start=True, stop=True)
                pe.matmul(bank[2 * n + 1][:, 0:t1 - t0], onesf[0:W, :], stw[0:W, t0:t1], start=True, stop=True
                          ).then_inc(meta_ps, 1)

            pe.wait_ge(bd_done, 1)
            pe.wait_ge(meta_sb, len(cuts))
            with pe.Fori(0, W) as i:
                pe.wait_ge(a_qs, i + 1)
                for h in range(2):
                    mm = pe.matmul(bank[5][:, 0:D + H], qs[:, h, :], bd[:, h, :], start=(h == 0), stop=(h == 1))
                mm.then_inc(a_num, 1)
                pe.wait_ge(a_att, i + 1)
                for h in range(2):
                    mm = pe.transpose(bank[6][:, h * P:(h + 1) * P], att[:, h * P:(h + 1) * P], ident[:, :])
                mm.then_inc(a_at, 1)
                pe.wait_ge(a_attT, i + 1)
                for h in range(2):
                    mm = pe.matmul(bank[7][:, 0:D], attT[:, h, :], wpT[:, h, :], start=(h == 0), stop=(h == 1))
                mm.then_inc(a_pj, 1)
                pe.wait_ge(a_mix, i + 1)

            def turn(g, b):
                pe.wait_ge(e_V, g + 1)
                for j in range(GT):
                    mm = pe.transpose(bank[0][:, j * P:(j + 1) * P], V[:, b, j, :], ident[:, :])
                mm.then_inc(e_VT, 1)

            def spread(g, b):
                pe.wait_ge(e_OT, g + 1)
                pe.wait_ge(e_R, g + 1)
                pe.wait_ge(e_pr, g + 1)
                for j in range(GT):
                    mm = pe.matmul(bank[1][:, 2 * j:2 * j + 2], OT[:, b, j, :], pr[:, b, j, :], start=True, stop=True)
                mm.then_inc(e_EX, 1)

            def total(g, b, r, j, freed=True):
                pe.wait_ge(e_S, g + 1)
                if freed:
                    pe.wait_ge(e_U, g * GT + (j - 1))
                pe.matmul(bank[2 + j % 2][:, 0:D + 1], S[:, b, j, :], G[:, r, j, 0:D + 1], start=True, stop=True
                          ).then_inc(e_A, 1)

            pe.wait_ge(table_out, 16)
            turn(0, 0)
            spread(0, 0)

            def step(g, r, first=False):
                for j in range(GT):
                    if j == 2:
                        turn(g + 1, (r + 1) % 2)
                    total(g, r % 2, r, j, not first or j >= 2)
                spread(g + 1, (r + 1) % 2)

            for r in range(GR):
                step(r, r, r == 0)
            with pe.Fori(1, NG // GR) as i:
                for r in range(GR):
                    step(i * GR + r, r)

            pe.wait_ge(loaded["experts"], 32)
            with pe.Fori(0, W) as i:
                pe.wait_ge(m_x2, i + 1)
                for h in range(2):
                    mm = pe.transpose(bank[0][:, h * P:(h + 1) * P], x2[:, h * P:(h + 1) * P], ident[:, :])
                mm.then_inc(m_xt, 1)
                pe.wait_ge(m_xtc, i + 1)
                for h in range(2):
                    mm = pe.matmul(bank[1][:, 0:X], x2T[:, h, :], rwT[:, h, :], start=(h == 0), stop=(h == 1))
                mm.then_inc(m_lg, 1)

                def up(e):
                    if e >= 2:
                        pe.wait_ge(m_gl, i * (2 * X) + 2 * (e - 1))
                    for f in range(2):
                        for h in range(2):
                            mm = pe.matmul(bank[4 + e % 2][:, f * P:(f + 1) * P], w1s[:, e, h, f * P:(f + 1) * P],
                                           x2T[:, h, :], start=(h == 0), stop=(h == 1))
                    mm.then_inc(m_h, 1)

                def down(e):
                    pe.wait_ge(m_gl, i * (2 * X) + 2 * (e + 1))
                    if e >= 2:
                        pe.wait_ge(m_acc, i * X + (e - 1))
                    for f in range(2):
                        mm = pe.matmul(bank[6 + e % 2][:, 0:D], hT[:, e % 2, f, :], w2s[:, e, f, :], start=(f == 0),
                                       stop=(f == 1))
                    mm.then_inc(m_y, 1)

                pe.wait_ge(m_comb, i + 1)
                pe.transpose(bank[2][0:X, 0:P], comb[:, :], ident[:, :]).then_inc(m_ct, 1)
                up(0)
                for e in range(1, X):
                    up(e)
                    down(e - 1)
                down(X - 1)
                pe.wait_ge(m_ctc, i + 1)
                pe.wait_ge(m_acc, i * X + (X - 1))
                pe.matmul(bank[6][:, 0:D], combT[:, :], b2s[:, :], start=True, stop=True).then_inc(m_y, 1)

        @block.vector
        def _(dve):
            steps = [0]

            def link(ins):
                steps[0] += 1
                ins.then_inc(dv, 1)
                dve.wait_ge(dv, steps[0])

            def pause():
                dve.memset(idle[:, :], 0.0)

            dve.wait_ge(loaded["edges"], 16 * 6)
            dve.wait_ge(consts, 4)
            link(dve.tensor_scalar(slot[:, :], srci, 7, None, ALU.logical_shift_right))
            link(dve.tensor_copy(winb, slot[:, :]))
            dve.wait_ge(blank, 16)
            link(dve.tensor_scalar(rec[:, :, 1], srci, P - 1, None, ALU.bitwise_and))
            link(dve.tensor_copy(rec[:, :, 0], dsti))
            with dve.Fori(0, W) as i:
                dve.tensor_scalar(maskb, winb, iotap[:, ds(i, 1)], None, ALU.is_equal, ALU.add,
                                  accum_out=cnt[:, ds(i, 1)]).then_inc(counted, 1)
                dve.wait_ge(counted, i + 1)
            dve.wait_ge(prefix, 1)
            link(dve.tensor_scalar(nti[:, :], bank[7][:, 64:64 + W], float(P - 1), None, ALU.add))
            link(dve.tensor_scalar(nti[:, :], nti[:, :], 7, None, ALU.logical_shift_right))
            link(dve.tensor_scalar(ntf[:, :], nti[:, :], 1.0, None, ALU.max))
            link(dve.tensor_scalar(ntci[0:W, :], bank[7][0:W, 128:129], float(P - 1), None, ALU.add))
            link(dve.tensor_scalar(ntci[0:W, :], ntci[0:W, :], 7, None, ALU.logical_shift_right))
            dve.tensor_scalar(ntc[0:W, :], ntci[0:W, :], 1.0, None, ALU.max).then_inc(ntc_done, 1)
            dve.wait_ge(ntc_done, 1)
            link(dve.tensor_tensor_scan(tend[:, :], onesf[:, 0:W], ntf[:, :], 0.0, ALU.mult, ALU.add))
            link(dve.tensor_copy(tendi[:, 0:W], tend[:, :]))
            link(dve.memset(tendi[:, W:W + 1], 0))
            link(dve.tensor_tensor(ntf[:, :], tend[:, :], ntf[:, :], ALU.subtract))
            link(dve.scalar_tensor_tensor(base[:, :], ntf[:, :], float(P), bank[7][:, 0:W], ALU.mult, ALU.add))
            link(dve.tensor_scalar(base[:, :], base[:, :], -1.0, None, ALU.add))
            with dve.Fori(0, W) as i:
                dve.tensor_scalar(maskb, winb, iotap[:, ds(i, 1)], None, ALU.is_equal
                                  ).then_inc(ranked, 1)
                dve.wait_ge(ranked, i * 3 + 1)
                dve.tensor_tensor_scan(rank, onebf, maskb, base[:, ds(i, 1)], ALU.mult, ALU.add
                                       ).then_inc(ranked, 1)
                dve.wait_ge(ranked, i * 3 + 2)
                pause()
                dve.copy_predicated(posf, maskb.bitcast(U16), rank).then_inc(ranked, 1)
                dve.wait_ge(ranked, i * 3 + 3)
            link(dve.tensor_copy(slot[:, :], posf))
            link(dve.tensor_scalar(srci, slot[:, :], P - 1, None, ALU.bitwise_and))
            link(dve.tensor_scalar(slot[:, :], slot[:, :], 7, None, ALU.logical_shift_right))
            dve.scalar_tensor_tensor(slot[:, :], srci, float(TP), slot[:, :], ALU.mult, ALU.add
                                     ).then_inc(slot_done, 1)
            dve.wait_ge(prefix, 2)
            link(dve.tensor_copy(tsc[0:W, :], bank[6][0:W, 0:1]))
            link(dve.tensor_tensor(tec[0:W, :], tsc[0:W, :], ntc[0:W, :], ALU.add))
            dve.wait_ge(consts, 10)
            link(dve.tensor_scalar(stw[0:W, :], inw[0:W, :], tsc[0:W, :], None, ALU.is_ge))
            link(dve.scalar_tensor_tensor(stw[0:W, :], inw[0:W, :], tec[0:W, :], stw[0:W, :], ALU.is_lt, ALU.mult))
            link(dve.tensor_scalar(meta[0:W, :, 0], inw[0:W, :], tsc[0:W, :], None, ALU.is_equal))
            link(dve.tensor_copy(inw[0:W, :], stw[0:W, :]))
            link(dve.tensor_copy(stw[0:W, :], meta[0:W, :, 0]))

            dve.wait_ge(loaded["x"], 32)
            with dve.Fori(0, W) as i:
                dve.bn_stats(stats[:, :], xs[:, ds(i, 1), :].rearrange("p a c -> p (a c)")).then_inc(stat1, 1)
                dve.wait_ge(stat1, i + 1)
                pause()
                dve.bn_aggr(agg[:, :], stats[:, :]).then_inc(stat3, 1)
                dve.wait_ge(stat3, i + 1)
                dve.tensor_copy(mv[:, ds(i, 1), :].rearrange("p a c -> p (a c)"), agg[:, :]).then_inc(stat2, 1)
            dve.wait_ge(std_done, 1)
            dve.reciprocal(rs[:, :], sd[:, :]).then_inc(rstd_done, 1)
            dve.wait_ge(rstd_done, 1)
            link(dve.memset(tab[:, :, D:D + 1], 1.0))
            dve.wait_ge(loaded["weights"], 16 * 7)
            with dve.Fori(0, W) as i:
                dve.tensor_scalar(xn[:, :], xs[:, ds(i, 1), :].rearrange("p a c -> p (a c)"), mv[:, ds(i, 1), 0],
                                  rs[:, ds(i, 1)], ALU.subtract, ALU.mult).then_inc(n_xn, 1)
                row_i = tab[:, ds(i, 1), 0:D].rearrange("p a c -> p (a c)")
                dve.wait_ge(n_wh, i + 1)
                dve.tensor_tensor(row_i, bank[1][:, 0:D], wbb[:, :], ALU.add).then_inc(n_tab, 1)
                dve.wait_ge(n_tab, i + 1)
                dve.tensor_tensor(xn[:, :], row_i, adst[:, :], ALU.mult).then_inc(n_tab2, 1)
                dve.wait_ge(n_tab2, i * 2 + 1)
                dve.tensor_reduce(tab[:, ds(i, 1), D + 1], xn[:, :], AX.X, ALU.add).then_inc(n_fd, 1)
                dve.wait_ge(n_fd, i * 2 + 1)
                dve.tensor_tensor(xn[:, :], row_i, asrc[:, :], ALU.mult).then_inc(n_tab2, 1)
                dve.wait_ge(n_tab2, i * 2 + 2)
                dve.tensor_reduce(frc[:, ds(i, 1)], xn[:, :], AX.X, ALU.add).then_inc(n_fd, 1)
                dve.wait_ge(n_kraw, i + 1)
                dve.scalar_tensor_tensor(kk[:, :], ek[:, :], 1.0, rk[:, :], ALU.min, ALU.add).then_inc(n_kk, 1)
                dve.wait_ge(n_qraw, i + 1)
                dve.scalar_tensor_tensor(qT[:, :, ds(i * P, P)], eq[:, :].rearrange("p (h n) -> p h n", h=2), 1.0,
                                         rq[:, :].rearrange("p (h n) -> p h n", h=2), ALU.min, ALU.add
                                         ).then_inc(n_qT, 1)
                dve.wait_ge(n_fd, i * 2 + 2)

            dve.tensor_reduce(cmax[:, :], tab[:, :, D + 1], AX.X, ALU.max, apply_absolute_value=True
                              ).then_inc(c_in, 1)
            dve.wait_ge(c_ps, 1)
            dve.tensor_reduce(c1[:, :], bank[6][0:1, 0:P], AX.X, ALU.max).then_inc(c_in, 1)
            dve.wait_ge(c_ps, 2)
            link(dve.tensor_scalar(coff[:, :], bank[6][:, 0:1], 1.0, None, ALU.add))
            dve.wait_ge(c_ps, 3)
            dve.tensor_copy(frT[0:W, :], bank[7][0:W, 0:P]).then_inc(tiles_in, 1)
            link(dve.memset(bd[:, :, :], 0.0))
            dve.wait_ge(n_ctx, W)
            for hd in range(H):
                h, p = hd * DH // P, hd * DH % P
                dve.tensor_copy(bd[p:p + DH, h, hd * DH:(hd + 1) * DH], bank[4 + h][p:p + DH, hd * DH:(hd + 1) * DH])
                last = dve.tensor_copy(bd[p:p + DH, h, D + hd:D + hd + 1], bank[4 + h][p:p + DH, D:D + 1])
            last.then_inc(bd_done, 1)

            dve.wait_ge(table_out, 16)
            with dve.Fori(0, W) as i:
                x_i = xs[:, ds(i, 1), :].rearrange("p a c -> p (a c)")
                dve.wait_ge(a_num, i + 1)
                dve.tensor_scalar(dmx[:, :], bank[5][:, D:D + H], 1e-6, None, ALU.max).then_inc(a_dm, 1)
                dve.wait_ge(a_dm, i + 1)
                dve.reciprocal(dinv[:, :], dmx[:, :]).then_inc(a_di, 1)
                dve.wait_ge(a_di, i + 1)
                dve.tensor_tensor(att.rearrange("p (h d) -> p h d", h=H),
                                  bank[5][:, 0:D].rearrange("p (h d) -> p h d", h=H),
                                  dinv[:, :].rearrange("p (h a) -> p h a", a=1).to_broadcast([P, H, DH]), ALU.mult
                                  ).then_inc(a_att, 1)
                dve.wait_ge(a_pj, i + 1)
                dve.tensor_tensor(mixs, bank[7][:, 0:D], bpb[:, :], ALU.add).then_inc(a_mix, 1)
                dve.wait_ge(a_mix, i + 1)
                dve.tensor_tensor(x_i, x_i, mixs, ALU.add).then_inc(a_x, 1)
                dve.wait_ge(a_x, i + 1)

            last_tile = dve.alloc_register("last_tile")
            window = dve.alloc_register("window")
            dve.reg_mov(window, 0)
            dve.reg_load(last_tile, tendi[0:1, 0:1])
            link(dve.memset(U, 0.0))
            dve.wait_ge(meta_sb, len(cuts) + 1)

            def values(g, b, r, k):
                dve.wait_ge(rows_in[r], k)
                dve.wait_ge(e_m4, g + 1)
                dve.tensor_scalar(fdp[:, b, :], G[:, r, :, D + 1], coff[:, :], None, ALU.add).then_inc(e_fdp, 1)
                dve.wait_ge(e_fdp, g + 1)
                for j in range(GT):
                    ins = dve.tensor_scalar(V[:, b, j, :], iotap[:, :], m4[:, b, j, 2:3], fdp[:, b, j:j + 1],
                                            ALU.is_equal, ALU.mult)
                ins.then_inc(e_V, 1)

            def weights(g, b, r, first=False):
                dve.wait_ge(e_VT, g + 1)
                dve.tensor_reduce(mloc[:, b, :], bank[0][:, :].rearrange("p (j e) -> p j e", j=GT), AX.X, ALU.max
                                  ).then_inc(e_ml, 1)
                dve.wait_ge(e_ml, g + 1)
                dve.tensor_tensor_scan(mx[:, b, :], m4[:, b, :, 1], mloc[:, b, :],
                                       0.0 if first else mx[:, 1 - b, GT - 1:GT], ALU.mult, ALU.max
                                       ).then_inc(e_mx, 1)
                dve.wait_ge(e_mx, g + 1)
                dve.scalar_tensor_tensor(cc[:, b, :], mx[:, b, :], coff[:, :], m4[:, b, :, 0], ALU.subtract, ALU.add
                                         ).then_inc(e_cc, 1)
                dve.wait_ge(e_cc, g + 1)
                dve.scalar_tensor_tensor(pr[:, b, :, 1], cc[:, b, :], ALPHA, cc[:, b, :], ALU.mult, ALU.max
                                         ).then_inc(e_R, 1)
                dve.wait_ge(e_R, g + 1)
                if first:
                    dve.memset(gd[:, b, 0:1], 0.0)
                else:
                    dve.tensor_tensor(gd[:, b, 0:1], pr[:, 1 - b, GT - 1, 1:2], pr[:, b, 0, 1:2], ALU.subtract)
                dve.tensor_tensor(gd[:, b, 1:GT], pr[:, b, 0:GT - 1, 1], pr[:, b, 1:GT, 1], ALU.subtract
                                  ).then_inc(e_gd, 1)
                dve.wait_ge(e_gd, g + 1)
                dve.tensor_scalar(gc[:, b, :], gd[:, b, :], 0.0, None, ALU.min).then_inc(e_gc, 1)
                dve.wait_ge(e_EX, g + 1)
                ex_e = bank[1][:, 0:2 * GT].rearrange("p (j c) -> p j c", c=2)
                dve.tensor_tensor(s1[:, b, :], ex_e[:, :, 0], G[:, r, :, D + 1], ALU.add).then_inc(e_s1, 1)
                dve.wait_ge(e_s1, g + 1)
                dve.scalar_tensor_tensor(s2[:, b, :], s1[:, b, :], ALPHA, s1[:, b, :], ALU.mult, ALU.max
                                         ).then_inc(e_s2, 1)
                dve.wait_ge(e_s2, g + 1)
                dve.tensor_tensor(s3[:, b, :], s2[:, b, :], ex_e[:, :, 1], ALU.subtract).then_inc(e_s3, 1)
                dve.wait_ge(e_s3, g + 1)
                dve.tensor_scalar(s4[:, b, :], s3[:, b, :], 0.0, None, ALU.min).then_inc(e_s4, 1)
                dve.wait_ge(e_ge, g + 1)
                dve.tensor_tensor(gg[:, b, :], ge[:, b, :], m4[:, b, :, 1], ALU.mult).then_inc(e_gg, 1)
                dve.wait_ge(e_w4, g + 1)
                for j in range(GT):
                    ins = dve.tensor_scalar(S[:, b, j, :], iotap[:, :], m4[:, b, j, 2:3], w4[:, b, j:j + 1],
                                            ALU.is_equal, ALU.mult)
                ins.then_inc(e_S, 1)
                dve.wait_ge(e_S, g + 1)

            def add_up(g, b, first=False):
                for j in range(GT):
                    t = g * GT + j
                    if not (first and j == 0):
                        dve.wait_ge(e_U, t)
                    dve.wait_ge(e_A, t + 1)
                    dve.scalar_tensor_tensor(U, U, gg[:, b, j:j + 1], bank[2 + j % 2][:, 0:D + 1],
                                             ALU.mult, ALU.add).then_inc(e_U, 1)
                    with dve.If(dve.snap(last_tile) == t + 1):
                        w = dve.snap(window, min_val=0, max_val=W - 1)
                        dve.wait_ge(e_U, t + 1)
                        dve.tensor_scalar(dn[:, :], U[:, D:D + 1], 1e-30, None, ALU.max).then_inc(f_dn, 1)
                        dve.wait_ge(f_dn, w + 1)
                        dve.reciprocal(rd[:, :], dn[:, :]).then_inc(f_rd, 1)
                        dve.wait_ge(f_rd, w + 1)
                        dve.tensor_scalar(hh, U[:, 0:D], rd[:, :], 0.0, ALU.mult, ALU.max).then_inc(f_hh, 1)
                        dve.wait_ge(f_hh, w + 1)
                        x_w = xs[:, ds(w, 1), :].rearrange("p a c -> p (a c)")
                        dve.tensor_tensor(x_w, x_w, hh, ALU.add).then_inc(f_x, 1)
                        dve.wait_ge(f_x, w + 1)
                        pause()
                        dve.reg_load(last_tile, tendi[0:1, ds(w + 1, 1)])
                        dve.reg_add(window, window, 1)

            values(0, 0, 0, 16 * GT)
            weights(0, 0, 0, True)
            for r in range(GR):
                values(r + 1, (r + 1) % 2, (r + 1) % GR, 16 * GT * ((r + 1) // GR + 1))
                add_up(r, r % 2, r == 0)
                weights(r + 1, (r + 1) % 2, (r + 1) % GR)
            with dve.Fori(1, NG // GR) as i:
                for r in range(GR):
                    g = i * GR + r
                    values(g + 1, (r + 1) % 2, (r + 1) % GR, i * (16 * GT) + 16 * GT * ((r + 1) // GR + 1))
                    add_up(g, r % 2)
                    weights(g + 1, (r + 1) % 2, (r + 1) % GR)

            with dve.Fori(0, W) as i:
                dve.bn_stats(stats[:, :], xs[:, ds(i, 1), :].rearrange("p a c -> p (a c)")).then_inc(m_st, 1)
                dve.wait_ge(m_st, i + 1)
                pause()
                dve.bn_aggr(agg[:, :], stats[:, :]).then_inc(m_ag0, 1)
                dve.wait_ge(m_ag0, i + 1)
                dve.tensor_copy(mv[:, ds(i, 1), :].rearrange("p a c -> p (a c)"), agg[:, :]).then_inc(m_ag, 1)
            dve.wait_ge(m_sd, 1)
            dve.reciprocal(rs[:, :], sd[:, :]).then_inc(m_rs, 1)
            dve.wait_ge(m_rs, 1)
            NSM = 9
            with dve.Fori(0, W) as i:
                x_i = xs[:, ds(i, 1), :].rearrange("p a c -> p (a c)")
                dve.tensor_scalar(x2, x_i, mv[:, ds(i, 1), 0], rs[:, ds(i, 1)], ALU.subtract, ALU.mult
                                  ).then_inc(m_x2, 1)
                dve.wait_ge(m_x2, i + 1)
                dve.tensor_tensor(acc, x_i, x2, ALU.add).then_inc(m_acc0, 1)
                dve.wait_ge(m_lg, i + 1)
                dve.tensor_copy(lg[:, :], bank[1][:, 0:X]).then_inc(m_lgc, 1)
                dve.wait_ge(m_lgc, i + 1)
                pause()
                dve.max(mx8[:, :], lg[:, :]).then_inc(m_mx, 1)
                dve.wait_ge(m_mx, i + 1)
                dve.tensor_scalar(nm[:, :], mx8[:, 0:1], -1.0, None, ALU.mult).then_inc(m_nm, 1)
                pause()
                dve.max_index(ix8[:, :], mx8[:, :], lg[:, :]).then_inc(m_ix, 1)
                dve.wait_ge(m_ix, i + 1)
                n = [0]

                def small(ins):
                    n[0] += 1
                    ins.then_inc(m_small, 1)
                    dve.wait_ge(m_small, i * NSM + n[0])

                small(dve.tensor_copy(ixf[:, :], ix8[:, :]))
                dve.wait_ge(m_ex, i + 1)
                small(dve.reciprocal(rsm[:, :], sm[:, :]))
                small(dve.tensor_scalar(p8[:, :], e8[:, :], rsm[:, :], None, ALU.mult))
                small(dve.tensor_tensor(tot[:, :], p8[:, 0:1], p8[:, 1:2], ALU.add))
                small(dve.tensor_scalar(totc[:, :], tot[:, :], 1e-12, None, ALU.max))
                small(dve.reciprocal(rt[:, :], totc[:, :]))
                small(dve.tensor_scalar(ww[:, :], p8[:, 0:2], rt[:, :], None, ALU.mult))
                small(dve.tensor_scalar(cA[:, :], iotap[:, 0:X], ixf[:, 0:1], ww[:, 0:1], ALU.is_equal, ALU.mult))
                small(dve.tensor_scalar(cB[:, :], iotap[:, 0:X], ixf[:, 1:2], ww[:, 1:2], ALU.is_equal, ALU.mult))
                assert n[0] == NSM
                dve.tensor_tensor(comb[:, :], cA[:, :], cB[:, :], ALU.add).then_inc(m_comb, 1)
                dve.wait_ge(m_comb, i + 1)
                for e in range(X):
                    dve.wait_ge(m_y, i * (X + 1) + (e + 1))
                    dve.scalar_tensor_tensor(acc, bank[6 + e % 2][:, 0:D], comb[:, e:e + 1], acc,
                                             ALU.mult, ALU.add).then_inc(m_acc, 1)
                    dve.wait_ge(m_acc, i * X + (e + 1))
                dve.wait_ge(m_y, i * (X + 1) + (X + 1))
                dve.tensor_tensor(x_i, bank[6][:, 0:D], acc, ALU.add).then_inc(m_res, 1)
                dve.wait_ge(m_res, i + 1)


_INS = ['x', 'src', 'dst', 'L0_gnn_W_w', 'L0_gnn_W_b', 'L0_gnn_a_w', 'L0_gnn_a_b', 'L0_mix_Wq', 'L0_mix_Wkv',
        'L0_mix_Wproj', 'L0_mix_bproj', 'L0_ffn_router_w', 'L0_ffn_w1', 'L0_ffn_b1', 'L0_ffn_w2', 'L0_ffn_b2']


def kernel(**inputs):
    import numpy as _np
    import concourse.bacc as _bacc
    from concourse import mybir as _mybir
    from concourse.bass_utils import run_bass_kernel_spmd as _run

    nc = _bacc.Bacc("TRN2", target_bir_lowering=False, num_devices=1)
    arrays, args = {}, []
    for name in _INS:
        a = _np.ascontiguousarray(inputs[name])
        arrays[f"in_{name}_dram"] = a
        args.append(nc.dram_tensor(f"in_{name}_dram", a.shape, _mybir.dt.from_np(a.dtype), kind="ExternalInput").ap())
    shape = inputs['x'].shape
    args.append(nc.dram_tensor("out_dram", shape, _mybir.dt.float32, kind="ExternalOutput").ap())
    graph_layer(nc, *args)
    return _run(nc, [arrays], core_ids=[0]).results[0]["out_dram"]
```

```python
from contextlib import ExitStack

import concourse.bass as bass
from concourse import mybir

F32 = mybir.dt.float32
I32 = mybir.dt.int32
U16 = mybir.dt.uint16
BF16 = mybir.dt.bfloat16
F16 = mybir.dt.float16
ALU = mybir.AluOpType
ACT = mybir.ActivationFunctionType
AX = mybir.AxisListType

P = 128
ds = bass.ds


def graph_layer(nc, x, src, dst, W_w, W_b, a_w, a_b, Wq, Wkv, Wproj, bproj, router_w, w1, b1, w2, b2, out):
    N, D = x.shape
    E = src.shape[0]
    X = router_w.shape[0]
    H = 8
    DH = D // H
    ALPHA = 0.2
    W = -(-N // P)
    LAST = N - (W - 1) * P
    EC = -(-E // P)
    EFULL = E // EC
    EREST = E - EFULL * EC
    GT = 4
    GE = GT * P
    GR = 4
    NG = (E + (GE - 1) * W + W - 1) // GE
    NG = -(-NG // GR) * GR
    AHEAD = 2
    T = NG * GT
    TP = T + max(-(-EC // P), AHEAD * GT)
    SC = 16
    SH = SC // 2
    TW = D + 2
    MG = NG + AHEAD
    NB = 4
    FULL = (W - 1) // NB
    REST = W - FULL * NB
    SV = 2

    table = nc.dram_tensor("table", [W * P, TW], F32).ap()
    binned = nc.dram_tensor("binned", [P * TP, 2], I32).ap()

    with ExitStack() as ctx:
        def sb(name, shape, dt=F32):
            return ctx.enter_context(nc.sbuf_tensor(name, shape, dt))

        def sem(name):
            return ctx.enter_context(nc.semaphore(name))

        xs = sb("xs", [P, W, D])
        work = sb("work", [P, W * TW])
        tab = work[:, :].rearrange("p (w c) -> p w c", w=W)
        place = [0]

        def part(*shape):
            n = 1
            for k in shape:
                n *= k
            a, place[0] = place[0], place[0] + n
            assert place[0] <= W * TW
            names = [f"d{k}" for k in range(len(shape))]
            v = work[:, a:a + n]
            if len(shape) > 1:
                v = v.rearrange(f"p ({' '.join(names)}) -> p {' '.join(names)}", **dict(zip(names, shape)))
            return v

        big = sb("big", [P, 2 * W * P])
        qT = big[:, :].rearrange("p (h n) -> p h n", h=2)
        WE = X * 2 * D
        wparts = [big[:, n * WE // 2:(n + 1) * WE // 2].bitcast(F16).rearrange("p (e h f) -> p e h f", e=X, h=2)
                  for n in range(4)]
        w1p, w2p = wparts[0:2], wparts[2:4]
        free = 2 * WE
        stagew = big[:, free:free + WE]
        stagew_e = stagew.rearrange("p (e h f) -> p e h f", e=X, h=2)
        stageb = big[0:33, free:free + X * D]
        hT = big[:, free:free + 2 * NB * P].rearrange("p (f n) -> p f n", f=2)
        free += 2 * NB * P
        hTp = []
        for n in range(2):
            hTp.append(big[:, free:free + 2 * NB * P].bitcast(F16).rearrange("p (b f n) -> p b f n", b=2, f=2))
            free += 2 * NB * P
        b2p = big[0:33, free:free + X * D // 2].bitcast(F16)
        onesh = big[0:33, free + X * D // 2:free + X * D // 2 + P // 2].bitcast(F16)
        assert free + X * D // 2 + P // 2 <= 2 * W * P
        wraw = big[:, 0:8 * D].rearrange("p (n c) -> p n c", n=8)
        b1r = big[0:X, 8 * D:9 * D]
        rws = big[0:X, 9 * D:10 * D]
        b1c = sb("b1c", [P, 2, X])
        rwT = sb("rwT", [P, 2, X])
        wws = sb("wws", [P, 2, D])
        wkvT = sb("wkvT", [P, 2, 2 * D])
        wqT = sb("wqT", [P, 2, D])
        wpT = sb("wpT", [P, 2, D])
        wbb = sb("wbb", [P, D])
        adst = sb("adst", [P, D])
        asrc = sb("asrc", [P, D])
        abb = sb("abb", [P, 1])
        bpb = sb("bpb", [P, D])
        ident = sb("ident", [P, P])
        onesf = sb("onesf", [P, P])
        before = sb("before", [P, P])
        iotap = sb("iotap", [P, P])
        iotab = sb("iotab", [P, P], BF16)
        valid = sb("valid", [P, W])
        epsc = sb("epsc", [P, 1])
        srci = part(EC).bitcast(I32)
        dsti = part(EC).bitcast(I32)
        rank = part(EC)
        posf = part(EC)
        winb = part(EC // 2).bitcast(BF16)
        maskb = part(EC // 2).bitcast(BF16)
        onebf = part(EC // 2).bitcast(BF16)
        slot = sb("slot", [P, EC], I32)
        lst = sb("lst", [P, TP, 2], I32)
        rec = lst[:, 0:EC, :]
        lst_f = lst[:, :, :].rearrange("p t c -> p (t c)").bitcast(F32)
        cnt = sb("cnt", [P, W])
        ntf = sb("ntf", [P, W])
        nti = sb("nti", [P, W], I32)
        tend = sb("tend", [P, W])
        tendi = sb("tendi", [P, W + 1], I32)
        base = sb("base", [P, W])
        ntc = sb("ntc", [64, 1])
        ntci = sb("ntci", [64, 1], I32)
        tec = sb("tec", [64, 1])
        tsc = sb("tsc", [64, 1])
        sidx = sb("sidx", [P, 2, SH], I32)
        srec = sb("srec", [P, 2, SH, 2], I32)
        stats = sb("stats", [P, 6])
        agg = sb("agg", [P, 2])
        idle = sb("idle", [P, 1])
        rest = sb("rest", [P, 1])
        mv = sb("mv", [P, W, 2])
        sd = sb("sd", [P, W])
        rs = sb("rs", [P, W])
        xn = sb("xn", [P, D])
        xnT = sb("xnT", [P, 2, P])
        frc = sb("frc", [P, W])
        ek = sb("ek", [P, D])
        rk = sb("rk", [P, D])
        kk = sb("kk", [P, D])
        vv = sb("vv", [P, D + 1])
        eq = sb("eq", [P, D])
        rq = sb("rq", [P, D])
        cmax = sb("cmax", [P, 1])
        c1 = sb("c1", [1, 1])
        coff = sb("coff", [P, 1])
        frT = sb("frT", [64, P])
        inw = sb("inw", [64, MG])
        startw = sb("startw", [64, MG])
        stw = sb("stw", [64, MG])
        meta = sb("meta", [P, MG, GT + 2])
        bd = sb("bd", [P, 2, D + H])
        dinv = sb("dinv", [P, H])
        dmx = sb("dmx", [P, H])
        gidx = sb("gidx", [P, GR, GT], I32)
        place[0] = 0
        G = part(GR, GT, TW)
        hot = part(2, GT, P // 2).bitcast(BF16)
        V = part(2, GT, P)
        OT = part(2, GT, P)
        S = part(2, GT, P)
        qs = part(2, P)
        att = part(D)
        attT = part(2, P)
        mixs = part(D)
        U = part(D + 1)
        hh = part(D)
        x2p = [work[:, n * W * P:(n + 1) * W * P].bitcast(F16).rearrange("p (h n) -> p h n", h=2) for n in range(2)]
        m4 = sb("m4", [P, GR, GT + 3])
        fdp = sb("fdp", [P, GR, GT])
        mloc = sb("mloc", [P, GR])
        mx = sb("mx", [P, GR])
        cc = sb("cc", [P, GR])
        pr = m4[:, :, GT + 1:GT + 3]
        gc = sb("gc", [P, GR])
        ge = sb("ge", [P, GR])
        gg = sb("gg", [P, GR])
        s1 = sb("s1", [P, GR, GT])
        s2 = sb("s2", [P, GR, GT])
        s3 = sb("s3", [P, GR, GT])
        s4 = sb("s4", [P, GR, GT])
        w4 = sb("w4", [P, GR, GT])
        dn = sb("dn", [P, 1])
        rd = sb("rd", [P, 1])
        lg, ex, sc, one1, one2 = (lst_f[:, n * W * X:(n + 1) * W * X].rearrange("p (w e) -> p w e", e=X)
                                  for n in range(5))
        comb = slot[:, 0:W * X].bitcast(F32).rearrange("p (w e) -> p w e", e=X)
        from_end = sb("from_end", [P, X])
        started = sb("started", [P, 5])
        top, key, tot, rt = cnt, ntf, tend, base

        bank = [ctx.enter_context(nc.psum_tensor(f"bank{n}", [P, 512], F32)) for n in range(8)]

        loaded = {n: sem("loaded_" + n) for n in ("edges", "x", "raw", "weights", "experts", "list")}
        filled = sem("filled")
        consts = sem("consts")
        masks = sem("masks")
        blank = sem("blank")
        dv = sem("dv")
        counted, ranked = sem("counted"), sem("ranked")
        prefix, ntc_done, slot_done = sem("prefix"), sem("ntc_done"), sem("slot_done")
        staged = [sem(f"staged{i}") for i in range(2)]
        scattered = [sem(f"scattered{i}") for i in range(2)]
        wt_ps, wt_sb = sem("wt_ps"), sem("wt_sb")
        stat1, stat2, stat3, std_done, rstd_done = sem("stat1"), sem("stat2"), sem("stat3"), sem("std_done"), sem("rstd_done")
        n_xn, n_xt, n_xnT, n_wh, n_kv, n_q, n_tab, n_tab2, n_fd, n_kraw, n_kk, n_qraw, n_qT, n_ctx = (
            sem("n_" + k) for k in ("xn", "xt", "xnT", "wh", "kv", "q", "tab", "tab2", "fd", "kraw", "kk", "qraw", "qT",
                                    "ctx"))
        ctx_zero = sem("ctx_zero")
        table_out = sem("table_out")
        c_in, c_ps = sem("c_in"), sem("c_ps")
        tiles_in, meta_ps, meta_sb = sem("tiles_in"), sem("meta_ps"), sem("meta_sb")
        bd_done = sem("bd_done")
        a_qs, a_num, a_dm, a_di, a_att, a_at, a_attT, a_pj, a_mix, a_x = (
            sem("a_" + k) for k in ("qs", "num", "dm", "di", "att", "at", "attT", "pj", "mix", "x"))
        listed = [sem(f"listed{i}") for i in range(GR)]
        rows_in = [sem(f"rows_in{i}") for i in range(GR)]
        (e_m4, e_fdp, e_hot, e_V, e_VT, e_ml, e_mx, e_cc, e_R, e_gc, e_ge, e_gg, e_OT, e_EX, e_s1, e_s2,
         e_s3, e_s4, e_w4, e_Sa, e_S, e_A, e_U) = (sem("e_" + k) for k in (
             "m4", "fdp", "hot", "V", "VT", "ml", "mx", "cc", "R", "gc", "ge", "gg", "OT", "EX", "s1", "s2",
             "s3", "s4", "w4", "Sa", "S", "A", "U"))
        f_dn, f_rd, f_hh, f_x = (sem("f_" + k) for k in ("dn", "rd", "hh", "x"))
        w_hi, w_lo, b_parts = sem("w_hi"), sem("w_lo"), sem("b_parts")
        m_st, m_ag0, m_ag, m_sd, m_rs, m_x2, m_x1, m_xt, m_xhi, m_xlo, m_lg, m_diff, m_ex, m_comb = (
            sem("m_" + k) for k in ("st", "ag0", "ag", "sd", "rs", "x2", "x1", "xt", "xhi", "xlo", "lg", "diff", "ex",
                                    "comb"))
        m_up, m_gelu, m_hi, m_lo, m_y, m_acc, m_out = (
            sem("m_" + k) for k in ("up", "gelu", "hi", "lo", "y", "acc", "out"))

        binned_p = binned.rearrange("(p t) c -> p t c", t=TP)
        assert MG <= 512
        turned = (0, 6)

        def row(a, n):
            return a.rearrange("(a n) -> a n", a=1).to_broadcast([n, a.shape[0]])

        block = ctx.enter_context(nc.Block())

        @block.sync
        def _(sp):
            sp.wait_ge(filled, 2)
            a = EFULL // 16 * 16
            for arr, buf in ((src, srci), (dst, dsti)):
                sp.dma_start(buf[0:a, :], arr[0:a * EC].rearrange("(p c) -> p c", c=EC)).then_inc(loaded["edges"], 16)
                sp.dma_start(buf[a:EFULL, :], arr[a * EC:EFULL * EC].rearrange("(p c) -> p c", c=EC)
                             ).then_inc(loaded["edges"], 16)
                sp.dma_start(buf[EFULL:EFULL + 1, 0:EREST], arr[EFULL * EC:E].rearrange("(p c) -> p c", p=1)
                             ).then_inc(loaded["edges"], 16)
            sp.wait_ge(filled, 3)
            sp.dma_start(xs[:, 0:W - 1, :], x[0:(W - 1) * P, :].rearrange("(w p) c -> p w c", p=P)
                         ).then_inc(loaded["x"], 16)
            sp.dma_start(xs[0:LAST, W - 1, :], x[(W - 1) * P:N, :]).then_inc(loaded["x"], 16)
            sp.wait_ge(filled, 5)
            sp.dma_start(binned_p, lst[:, :, :]).then_inc(blank, 16)
            sp.dma_start(wraw[:, 0:2, :], Wq.rearrange("(h p) c -> p h c", p=P)).then_inc(loaded["raw"], 16)
            sp.dma_start(wraw[:, 2:6, :], Wkv.rearrange("(h p) c -> p h c", p=P)).then_inc(loaded["raw"], 16)
            sp.dma_start(wraw[:, 6:8, :], Wproj.rearrange("(h p) c -> p h c", p=P)).then_inc(loaded["raw"], 16)
            sp.dma_start(rws, router_w).then_inc(loaded["raw"], 16)
            sp.dma_start(b1r, b1).then_inc(loaded["raw"], 16)
            sp.dma_start(wws[:, :, :], W_w.rearrange("(h p) c -> p h c", p=P)).then_inc(loaded["weights"], 16)
            sp.dma_start(wbb[:, :], row(W_b, P)).then_inc(loaded["weights"], 16)
            sp.dma_start(adst[:, :], row(a_w[0:D], P)).then_inc(loaded["weights"], 16)
            sp.dma_start(asrc[:, :], row(a_w[D:2 * D], P)).then_inc(loaded["weights"], 16)
            sp.dma_start(abb[:, :], row(a_b, P)).then_inc(loaded["weights"], 16)
            sp.dma_start(bpb[:, :], row(bproj, P)).then_inc(loaded["weights"], 16)
            sp.wait_ge(n_fd, 2 * W)
            sp.dma_start(table.rearrange("(w p) c -> p w c", p=P), tab[:, :, :]).then_inc(table_out, 16)
            sp.wait_ge(a_qs, W)
            sp.dma_start(stagew_e, w1.rearrange("e (h p) f -> p e h f", p=P)).then_inc(loaded["experts"], 16)
            sp.wait_ge(w_hi, 1)
            sp.wait_ge(w_lo, 1)
            sp.dma_start(stagew_e, w2.rearrange("e (h p) f -> p e h f", p=P)).then_inc(loaded["experts"], 16)
            sp.wait_ge(w_hi, 2)
            sp.wait_ge(w_lo, 2)
            for n in (0, 32):
                sp.dma_start(stageb[n:n + 1, :], b2.rearrange("(a e) d -> a (e d)", a=1)
                             ).then_inc(loaded["experts"], 16)
            sp.wait_ge(scattered[0], 16 * (SH * (EC // SC) + min(SH, EC % SC)))
            sp.wait_ge(scattered[1], 16 * (SH * (EC // SC) + max(0, EC % SC - SH)))
            sp.dma_start(lst[:, :, :], binned_p).then_inc(loaded["list"], 16)
            def result(i, n):
                rows = ds(i * (NB * P), n * P)
                sp.dma_start(out[rows, :].rearrange("(w p) c -> p w c", p=P), xs[:, ds(i * NB, n), :]
                             ).then_inc(m_out, 16)

            with sp.Fori(0, FULL) as i:
                sp.wait_ge(m_acc, i * (NB * X) + (NB * X + NB))
                result(i, NB)
            sp.wait_ge(m_acc, FULL * NB * X + REST * X + NB)
            if REST > 1:
                result(FULL, REST - 1)
            sp.dma_start(out[(W - 1) * P:N, :], xs[0:LAST, W - 1, :]).then_inc(m_out, 16)
            sp.wait_ge(m_out, 16 * (FULL + min(REST, 2)))

        @block.gpsimd
        def _(pool):
            pool.memset(srci, (W + 1) * P).then_inc(filled, 1)
            pool.memset(dsti, 0).then_inc(filled, 1)
            pool.memset(xs[:, W - 1, :], 0.0).then_inc(filled, 1)
            pool.memset(lst[:, :, 0], 0).then_inc(filled, 1)
            pool.memset(lst[:, :, 1], -1).then_inc(filled, 1)
            pool.iota(posf, pattern=[[1, EC]], base=T * P, channel_multiplier=0,
                      allow_small_or_imprecise_dtypes=True).then_inc(consts, 1)
            pool.iota(iotap[:, :], pattern=[[1, P]], base=0, channel_multiplier=0,
                      allow_small_or_imprecise_dtypes=True).then_inc(consts, 1)
            pool.iota(iotab[:, :], pattern=[[1, P]], base=0, channel_multiplier=0,
                      allow_small_or_imprecise_dtypes=True).then_inc(consts, 1)
            pool.memset(onesf[:, :], 1.0).then_inc(consts, 1)
            pool.memset(onebf, 1.0).then_inc(consts, 1)
            pool.memset(before[:, :], 1.0).then_inc(masks, 1)
            pool.memset(ident[:, :], 0.0).then_inc(masks, 1)
            pool.memset(valid[:, :], 1.0).then_inc(masks, 1)
            pool.wait_ge(masks, 3)
            pool.affine_select(out=before[:, :], in_=before[:, :], compare_op=ALU.is_gt, fill=0.0, base=0,
                               pattern=[[1, P]], channel_multiplier=-1).then_inc(consts, 1)
            pool.affine_select(out=ident[:, :], in_=ident[:, :], compare_op=ALU.not_equal, fill=1.0, base=0,
                               pattern=[[-1, P]], channel_multiplier=1).then_inc(consts, 1)
            pool.affine_select(out=valid[:, W - 1:W], in_=valid[:, W - 1:W], compare_op=ALU.is_gt, fill=0.0,
                               base=LAST, pattern=[[0, 1]], channel_multiplier=-1).then_inc(consts, 1)
            pool.memset(kk[:, 0:P], 0.0).then_inc(consts, 1)
            pool.memset(epsc[:, :], 1e-5).then_inc(consts, 1)
            pool.iota(inw[:, :], pattern=[[1, MG]], base=0, channel_multiplier=0,
                      allow_small_or_imprecise_dtypes=True).then_inc(consts, 1)

            pool.iota(from_end[:, :], pattern=[[-1, X]], base=X, channel_multiplier=0,
                      allow_small_or_imprecise_dtypes=True).then_inc(consts, 1)

            pool.wait_ge(slot_done, 1)
            pool.wait_ge(blank, 16)

            def stage(c, n, b):
                pool.tensor_copy(sidx[:, b, 0:n], slot[:, c]).then_inc(staged[b], 1)
                pool.tensor_copy(srec[:, b, 0:n, :], rec[:, c, :]).then_inc(staged[b], 1)

            def scatter(b, n):
                pool.tensor_tensor(rest[:, :], iotap[:, 0:1], iotap[:, 0:1], ALU.add)
                for j in range(n):
                    pool.indirect_dma_start(binned, bass.IndirectOffsetOnAxis(ap=sidx[:, b, j:j + 1], axis=0),
                                            srec[:, b, j, :], None).then_inc(scattered[b], 16)

            for b in range(2):
                stage(slice(b * SH, (b + 1) * SH), SH, b)
                pool.wait_ge(staged[b], 2)
                scatter(b, SH)
            full = EC // SC
            with pool.Fori(1, full) as i:
                for b in range(2):
                    pool.wait_ge(scattered[b], i * (16 * SH))
                    stage(ds(i * SC + b * SH, SH), SH, b)
                    pool.wait_ge(staged[b], i * 2 + 2)
                    scatter(b, SH)
            for b in range(2):
                n = min(SH, EC - full * SC - b * SH)
                if n > 0:
                    pool.wait_ge(scattered[b], full * 16 * SH)
                    stage(slice(full * SC + b * SH, full * SC + b * SH + n), n, b)
                    pool.wait_ge(staged[b], full * 2 + 2)
                    scatter(b, n)

            pool.wait_ge(loaded["list"], 16)
            pool.wait_ge(table_out, 16)
            pool.wait_ge(c_in, 1)

            def gather(r, c, k):
                pool.tensor_copy(gidx[:, r, :], lst[:, c, 0]).then_inc(listed[r], 1)
                pool.wait_ge(listed[r], k)
                pool.tensor_tensor(rest[:, :], iotap[:, 0:1], iotap[:, 0:1], ALU.add)
                for j in range(GT):
                    pool.indirect_dma_start(G[:, r, j, :], None, table,
                                            bass.IndirectOffsetOnAxis(ap=gidx[:, r, j:j + 1], axis=0)
                                            ).then_inc(rows_in[r], 16)

            pool.wait_ge(a_x, W)
            for r in range(GR):
                gather(r, slice(r * GT, (r + 1) * GT), 1)
            with pool.Fori(1, NG // GR) as i:
                for r in range(GR):
                    pool.wait_ge(e_A, i * GR + (r + 1 - GR))
                    gather(r, ds(i * (GR * GT) + r * GT, GT), i + 1)
            for r in range(AHEAD):
                pool.wait_ge(e_A, NG + r + 1 - GR)
                gather(r, slice(T + r * GT, T + (r + 1) * GT), NG // GR + 1)
            for r in range(AHEAD):
                pool.wait_ge(rows_in[r], 16 * GT * (NG // GR + 1))

        @block.scalar
        def _(act):
            for n, o in enumerate((wqT[:, :, 0:P], wqT[:, :, P:D], wkvT[:, :, 0:P], wkvT[:, :, P:2 * P],
                                   wkvT[:, :, 2 * P:3 * P], wkvT[:, :, 3 * P:4 * P], wpT[:, :, 0:P],
                                   wpT[:, :, P:D])):
                act.wait_ge(wt_ps, n + 1)
                act.copy(o, bank[n][:, 0:D].rearrange("p (h c) -> p h c", h=2)).then_inc(wt_sb, 1)
            act.wait_ge(wt_ps, 9)
            act.copy(rwT[:, :, :], bank[0][:, 0:2 * X].rearrange("p (h c) -> p h c", h=2)).then_inc(wt_sb, 1)
            act.copy(b1c[:, :, :], bank[0][:, 2 * X:4 * X].rearrange("p (h e) -> p h e", h=2)).then_inc(wt_sb, 1)
            act.wait_ge(consts, 12)
            act.wait_ge(stat2, W)
            act.activation(sd[:, :], mv[:, :, 1], ACT.Sqrt, bias=epsc[:, :]).then_inc(std_done, 1)

            with act.Fori(0, W) as i:
                act.wait_ge(n_xt, i + 1)
                act.copy(xnT[:, :, :], bank[0][:, 0:D].rearrange("p (h c) -> p h c", h=2)).then_inc(n_xnT, 1)
                act.wait_ge(n_kv, i + 1)
                act.activation(ek[:, :], bank[2][:, 0:D], ACT.Exp)
                act.activation(rk[:, :], bank[2][:, 0:D], ACT.Relu)
                act.copy(vv[:, 0:D], bank[2][:, D:2 * D])
                act.copy(vv[:, D:D + 1], valid[:, ds(i, 1)]).then_inc(n_kraw, 1)
                act.wait_ge(n_q, i + 1)
                act.activation(eq[:, :], bank[3][:, 0:D], ACT.Exp)
                act.activation(rq[:, :], bank[3][:, 0:D], ACT.Relu).then_inc(n_qraw, 1)

            act.wait_ge(meta_ps, 1)
            act.activation(meta[:, :, GT + 1], bank[0][:, 0:MG], ACT.Identity, bias=abb[:, :])
            act.activation(meta[:, :, GT], bank[1][:, 0:MG], ACT.Copy, bias=1.0, scale=-1.0
                           ).then_inc(meta_sb, 1)

            act.wait_ge(table_out, 16)
            act.wait_ge(bd_done, 1)
            with act.Fori(0, W) as i:
                act.copy(qs[:, :, :], qT[:, :, ds(i * P, P)]).then_inc(a_qs, 1)
                act.wait_ge(a_at, i + 1)
                act.copy(attT[:, :, :], bank[6][:, 0:D].rearrange("p (h c) -> p h c", h=2)).then_inc(a_attT, 1)
                act.wait_ge(a_pj, i + 1)

            for n in range(2):
                act.wait_ge(loaded["experts"], 16 * (n + 1))
                act.copy(wparts[2 * n], stagew_e).then_inc(w_hi, 1)

            act.wait_ge(loaded["list"], 16)
            act.copy(meta[:, :, 0:GT], lst[:, 0:MG * GT, 1].rearrange("p (g j) -> p g j", j=GT)).then_inc(meta_sb, 1)
            act.wait_ge(meta_sb, 2)

            def group_data(g, r, c):
                act.copy(m4[:, r, 0:GT + 2], meta[:, c, :]).then_inc(e_m4, 1)

            def one_hot_turned(g):
                act.wait_ge(e_ml, g[0] + 1)
                b = g[1] % 2
                act.activation(OT[:, b, :, :], bank[turned[b]][:, :].rearrange("p (j e) -> p j e", j=GT), ACT.Sign
                               ).then_inc(e_OT, 1)

            def values(g):
                act.wait_ge(e_hot, g[0] + 1)
                b, r = g[1] % 2, g[1] % GR
                for j in range(GT):
                    ins = act.activation(V[:, b, j, :], hot[:, b, j, :], ACT.Copy, scale=fdp[:, r, j:j + 1])
                ins.then_inc(e_V, 1)

            def weights(g, freed=True):
                b, r = g[1] % 2, g[1] % GR
                act.wait_ge(e_gc, g[0] + 1)
                act.activation(ge[:, r:r + 1], gc[:, r:r + 1], ACT.Exp).then_inc(e_ge, 1)
                act.wait_ge(e_s4, g[0] + 1)
                act.activation(w4[:, r, :], s4[:, r, :], ACT.Exp).then_inc(e_w4, 1)
                act.wait_ge(e_w4, g[0] + 1)
                if freed:
                    act.wait_ge(e_A, g[0] - 1)
                for j in range(SV, GT):
                    ins = act.activation(S[:, b, j, :], hot[:, b, j, :], ACT.Copy, scale=w4[:, r, j:j + 1])
                ins.then_inc(e_S, 1)

            def at(g, d, r):
                return g + d, (r + d) % GR

            for g in range(3):
                group_data(g, g, slice(g, g + 1))
            values((0, 0))
            one_hot_turned((0, 0))
            values((1, 1))
            weights((0, 0), False)

            def step(g, r, c, first=False, more=True):
                if more:
                    act.wait_ge(e_gg, g)
                    group_data(g + 3, (r + 3) % GR, c)
                one_hot_turned(at(g, 1, r))
                values(at(g, 2, r))
                weights(at(g, 1, r), not (first and r == 0))

            for r in range(GR):
                if r == 0:
                    group_data(3, 3, slice(3, 4))
                step(r, r, slice(r + 3, r + 4), True, r > 0)
            with act.Fori(1, NG // GR - 1) as i:
                for r in range(GR):
                    step(i * GR + r, r, ds(i * GR + r + 3, 1))
            for r in range(GR):
                g = NG - GR + r
                step(g, r, slice(g + 3, g + 4), more=g + 3 < MG)

            act.wait_ge(m_ag, W)
            act.activation(sd[:, :], mv[:, :, 1], ACT.Sqrt, bias=epsc[:, :]).then_inc(m_sd, 1)
            with act.Fori(0, W) as i:
                act.wait_ge(m_xt, i + 1)
                act.wait_ge(m_xlo, i + 1)
                x2t = bank[0][:, 0:D].rearrange("p (h c) -> p h c", h=2)
                act.copy(x2p[0][:, :, ds(i * P, P)], x2t)
                act.copy(xnT[:, :, :], x2t).then_inc(m_xhi, 1)
            act.wait_ge(m_diff, 1)
            act.activation(ex, lg, ACT.Exp).then_inc(m_ex, 1)
            act.wait_ge(b_parts, 1)

            def hidden(k, b, e, n):
                act.wait_ge(m_up, k + 1)
                act.wait_ge(m_lo, k + 1)
                for f in range(2):
                    act.activation(hT[:, f, 0:n * P], bank[4 + 2 * b + f][:, 0:n * P], ACT.Gelu,
                                   bias=b1c[:, f, e:e + 1]).then_inc(m_gelu, 1)
                act.wait_ge(m_gelu, k * 2 + 6)
                act.copy(hTp[0][:, b, :, 0:n * P], hT[:, :, 0:n * P]).then_inc(m_hi, 1)

            with act.Fori(0, FULL) as i:
                for e in range(X):
                    act.wait_ge(m_y, i * (NB * X) + (NB * e + NB))
                    hidden(i * X + e, e % 2, e, NB)
            for e in range(X):
                act.wait_ge(m_y, 2 * NB + FULL * NB * X + (REST * (e - 1) if e else -NB))
                hidden(FULL * X + e, e % 2, e, REST)

        @block.tensor
        def _(pe):
            pe.wait_ge(consts, 12)
            pe.wait_ge(loaded["raw"], 16 * 5)
            for n in range(8):
                for h in range(2):
                    mm = pe.transpose(bank[n][:, h * P:(h + 1) * P], wraw[:, n, h * P:(h + 1) * P], ident[:, :])
                mm.then_inc(wt_ps, 1)
            pe.wait_ge(wt_sb, 1)
            for h in range(2):
                pe.transpose(bank[0][:, h * X:(h + 1) * X], rws[:, h * P:(h + 1) * P], ident[0:X, 0:X])
                mm = pe.transpose(bank[0][:, (2 + h) * X:(3 + h) * X], b1r[:, h * P:(h + 1) * P], ident[0:X, 0:X])
            mm.then_inc(wt_ps, 1)
            pe.wait_ge(wt_sb, 10)
            pe.wait_ge(counted, W)
            pe.matmul(bank[7][:, 0:W], before[:, :], cnt[:, :], start=True, stop=True)
            pe.matmul(bank[7][:, 64:64 + W], onesf[:, :], cnt[:, :], start=True, stop=True)
            pe.matmul(bank[7][0:W, 128:129], cnt[:, :], onesf[:, 0:1], start=True, stop=True).then_inc(prefix, 1)
            pe.wait_ge(ntc_done, 1)
            pe.matmul(bank[6][0:W, 0:1], before[0:W, 0:W], ntc[0:W, :], start=True, stop=True).then_inc(prefix, 1)

            pe.wait_ge(loaded["weights"], 16 * 6)
            for h in range(2):
                pe.matmul(bank[4 + h][:, 0:D + 1], kk[:, 0:P], wkvT[:, 0, 0:D + 1], start=True, stop=True)
            with pe.Fori(0, W) as i:
                pe.wait_ge(n_xn, i + 1)
                for h in range(2):
                    mm = pe.transpose(bank[0][:, h * P:(h + 1) * P], xn[:, h * P:(h + 1) * P], ident[:, :])
                mm.then_inc(n_xt, 1)
                pe.wait_ge(n_xnT, i + 1)
                for h in range(2):
                    mm = pe.matmul(bank[1][:, 0:D], xnT[:, h, :], wws[:, h, :], start=(h == 0), stop=(h == 1))
                mm.then_inc(n_wh, 1)
                for h in range(2):
                    mm = pe.matmul(bank[2][:, :], xnT[:, h, :], wkvT[:, h, :], start=(h == 0), stop=(h == 1))
                mm.then_inc(n_kv, 1)
                for o in range(2):
                    for h in range(2):
                        mm = pe.matmul(bank[3][:, o * P:(o + 1) * P], wqT[:, h, o * P:(o + 1) * P], xnT[:, h, :],
                                       start=(h == 0), stop=(h == 1))
                mm.then_inc(n_q, 1)
                pe.wait_ge(n_kk, i + 1)
                pe.wait_ge(n_qT, i + 1)
                for h in range(2):
                    mm = pe.matmul(bank[4 + h][:, 0:D + 1], kk[:, h * P:(h + 1) * P], vv[:, :], start=False,
                                   stop=True, skip_group_check=True)
                mm.then_inc(n_ctx, 1)

            pe.wait_ge(c_in, 1)
            pe.transpose(bank[6][0:1, 0:P], cmax[:, :], ident[:, :]).then_inc(c_ps, 1)
            pe.wait_ge(c_in, 2)
            pe.matmul(bank[6][:, 0:1], onesf[0:1, :], c1[:, :], start=True, stop=True).then_inc(c_ps, 1)
            pe.transpose(bank[7][0:W, 0:P], frc[:, :], ident[:, :]).then_inc(c_ps, 1)
            pe.wait_ge(tiles_in, 1)
            pe.matmul(bank[0][:, 0:MG], frT[0:W, :], inw[0:W, :], start=True, stop=True)
            pe.matmul(bank[1][:, 0:MG], onesf[0:W, :], startw[0:W, :], start=True, stop=True).then_inc(meta_ps, 1)

            pe.wait_ge(bd_done, 1)
            pe.wait_ge(meta_sb, 1)
            with pe.Fori(0, W) as i:
                pe.wait_ge(a_qs, i + 1)
                for h in range(2):
                    mm = pe.matmul(bank[5][:, 0:D + H], qs[:, h, :], bd[:, h, :], start=(h == 0), stop=(h == 1))
                mm.then_inc(a_num, 1)
                pe.wait_ge(a_att, i + 1)
                for h in range(2):
                    mm = pe.transpose(bank[6][:, h * P:(h + 1) * P], att[:, h * P:(h + 1) * P], ident[:, :])
                mm.then_inc(a_at, 1)
                pe.wait_ge(a_attT, i + 1)
                for h in range(2):
                    mm = pe.matmul(bank[7][:, 0:D], attT[:, h, :], wpT[:, h, :], start=(h == 0), stop=(h == 1))
                mm.then_inc(a_pj, 1)
                pe.wait_ge(a_mix, i + 1)

            def turn(g, r):
                b = r % 2
                pe.wait_ge(e_V, g + 1)
                for j in range(GT):
                    mm = pe.transpose(bank[turned[b]][:, j * P:(j + 1) * P], V[:, b, j, :], ident[:, :])
                mm.then_inc(e_VT, 1)

            def spread(g, r):
                pe.wait_ge(e_OT, g + 1)
                pe.wait_ge(e_R, g + 1)
                pe.wait_ge(e_m4, g + 1)
                for j in range(GT):
                    mm = pe.matmul(bank[1][:, 2 * j:2 * j + 2], OT[:, r % 2, j, :], pr[:, r % GR, :], start=True,
                                   stop=True)
                mm.then_inc(e_EX, 1)

            def step(g, r, first=False):
                pe.wait_ge(e_Sa, g + 1)
                if not (first and r < 2):
                    pe.wait_ge(e_U, g - 1)
                for j in range(GT):
                    if j == 2:
                        spread(g + 1, r + 1)
                    if j == SV:
                        pe.wait_ge(e_S, g + 1)
                    mm = pe.matmul(bank[2 + r % 2][:, 0:D + 1], S[:, r % 2, j, :], G[:, r, j, 0:D + 1],
                                   start=(j == 0), stop=(j == GT - 1))
                mm.then_inc(e_A, 1)
                turn(g + 2, r + 2)

            pe.wait_ge(table_out, 16)
            turn(0, 0)
            turn(1, 1)
            spread(0, 0)
            for r in range(GR):
                step(r, r, True)
            with pe.Fori(1, NG // GR) as i:
                for r in range(GR):
                    step(i * GR + r, r)

            with pe.Fori(0, W) as i:
                pe.wait_ge(m_x2, i + 1)
                for h in range(2):
                    mm = pe.transpose(bank[0][:, h * P:(h + 1) * P], xn[:, h * P:(h + 1) * P], ident[:, :])
                mm.then_inc(m_xt, 1)
                pe.wait_ge(m_xhi, i + 1)
                for h in range(2):
                    mm = pe.matmul(bank[1][:, ds(i * X, X)], xnT[:, h, :], rwT[:, h, :], start=(h == 0),
                                   stop=(h == 1))
                mm.then_inc(m_lg, 1)

            PAIRS = ((0, 0), (0, 1), (1, 0))

            def up(k, b, e, i, n):
                pe.wait_ge(m_gelu, k * 2 + 2)
                for f in range(2):
                    for h in range(2):
                        for m, (pw, px) in enumerate(PAIRS):
                            mm = pe.matmul(bank[4 + 2 * b + f][:, 0:n * P], w1p[pw][:, e, h, f * P:(f + 1) * P],
                                           x2p[px][:, h, ds(i * (NB * P), n * P)], start=(h + m == 0),
                                           stop=(h == 1 and m == 2))
                mm.then_inc(m_up, 1)

            def down(k, y, b, e, n):
                pe.wait_ge(m_lo, k + 2)
                for j in range(n):
                    pe.wait_ge(m_acc, y + (NB - (n if e else NB) + j + 1))
                    pe.matmul(bank[j][:, 0:D], onesh, b2p[:, e * D:(e + 1) * D], start=True, stop=False)
                    for f in range(2):
                        for m, (ph, pw) in enumerate(PAIRS):
                            mm = pe.matmul(bank[j][:, 0:D], hTp[ph][:, b, f, j * P:(j + 1) * P], w2p[pw][:, e, f, :],
                                           start=False, stop=(f == 1 and m == 2))
                    mm.then_inc(m_y, 1)

            def batch(i, n, after):
                for e in range(X):
                    if e + 1 < X:
                        up(i * X + (e + 1), (e + 1) % 2, e + 1, i, n)
                    elif after:
                        up(i * X + (e + 1), (e + 1) % 2, 0, i + 1, after)
                    down(i * X + e, i * (NB * X) + n * e, e % 2, e, n)

            pe.wait_ge(b_parts, 1)
            pe.wait_ge(m_xlo, W + 1)
            up(0, 0, 0, 0, NB)
            with pe.Fori(0, FULL - 1) as i:
                batch(i, NB, NB)
            batch(FULL - 1, NB, REST)
            batch(FULL, REST, 0)

        @block.vector
        def _(dve):
            steps = [0]

            def link(ins):
                steps[0] += 1
                ins.then_inc(dv, 1)
                dve.wait_ge(dv, steps[0])

            def pause():
                dve.memset(idle[:, :], 0.0)

            dve.wait_ge(loaded["edges"], 16 * 6)
            dve.wait_ge(consts, 5)
            link(dve.tensor_scalar(slot[:, :], srci, 7, None, ALU.logical_shift_right))
            link(dve.tensor_copy(winb, slot[:, :]))
            dve.wait_ge(blank, 16)
            link(dve.tensor_scalar(rec[:, :, 1], srci, P - 1, None, ALU.bitwise_and))
            link(dve.tensor_copy(rec[:, :, 0], dsti))
            with dve.Fori(0, W) as i:
                dve.tensor_scalar(maskb, winb, iotap[:, ds(i, 1)], None, ALU.is_equal, ALU.add,
                                  accum_out=cnt[:, ds(i, 1)]).then_inc(counted, 1)
                dve.wait_ge(counted, i + 1)
            dve.wait_ge(prefix, 1)
            link(dve.tensor_scalar(nti[:, :], bank[7][:, 64:64 + W], float(GE - 1), None, ALU.add))
            link(dve.tensor_scalar(nti[:, :], nti[:, :], GE.bit_length() - 1, None, ALU.logical_shift_right))
            link(dve.tensor_scalar(ntf[:, :], nti[:, :], 1.0, None, ALU.max))
            link(dve.tensor_scalar(ntci[0:W, :], bank[7][0:W, 128:129], float(GE - 1), None, ALU.add))
            link(dve.tensor_scalar(ntci[0:W, :], ntci[0:W, :], GE.bit_length() - 1, None, ALU.logical_shift_right))
            dve.tensor_scalar(ntc[0:W, :], ntci[0:W, :], 1.0, None, ALU.max).then_inc(ntc_done, 1)
            dve.wait_ge(ntc_done, 1)
            link(dve.tensor_tensor_scan(tend[:, :], onesf[:, 0:W], ntf[:, :], 0.0, ALU.mult, ALU.add))
            link(dve.tensor_copy(tendi[:, 0:W], tend[:, :]))
            link(dve.memset(tendi[:, W:W + 1], 0))
            link(dve.tensor_tensor(ntf[:, :], tend[:, :], ntf[:, :], ALU.subtract))
            link(dve.scalar_tensor_tensor(base[:, :], ntf[:, :], float(GE), bank[7][:, 0:W], ALU.mult, ALU.add))
            link(dve.tensor_scalar(base[:, :], base[:, :], -1.0, None, ALU.add))
            with dve.Fori(0, W) as i:
                dve.tensor_scalar(maskb, winb, iotap[:, ds(i, 1)], None, ALU.is_equal
                                  ).then_inc(ranked, 1)
                dve.wait_ge(ranked, i * 3 + 1)
                dve.tensor_tensor_scan(rank, onebf, maskb, base[:, ds(i, 1)], ALU.mult, ALU.add
                                       ).then_inc(ranked, 1)
                dve.wait_ge(ranked, i * 3 + 2)
                pause()
                dve.copy_predicated(posf, maskb.bitcast(U16), rank).then_inc(ranked, 1)
                dve.wait_ge(ranked, i * 3 + 3)
            link(dve.tensor_copy(slot[:, :], posf))
            link(dve.tensor_scalar(srci, slot[:, :], P - 1, None, ALU.bitwise_and))
            link(dve.tensor_scalar(slot[:, :], slot[:, :], 7, None, ALU.logical_shift_right))
            dve.scalar_tensor_tensor(slot[:, :], srci, float(TP), slot[:, :], ALU.mult, ALU.add
                                     ).then_inc(slot_done, 1)
            dve.wait_ge(prefix, 2)
            link(dve.tensor_copy(tsc[0:W, :], bank[6][0:W, 0:1]))
            link(dve.tensor_tensor(tec[0:W, :], tsc[0:W, :], ntc[0:W, :], ALU.add))
            dve.wait_ge(consts, 12)
            link(dve.tensor_scalar(stw[0:W, :], inw[0:W, :], tsc[0:W, :], None, ALU.is_ge))
            link(dve.scalar_tensor_tensor(stw[0:W, :], inw[0:W, :], tec[0:W, :], stw[0:W, :], ALU.is_lt, ALU.mult))
            link(dve.tensor_scalar(startw[0:W, :], inw[0:W, :], tsc[0:W, :], None, ALU.is_equal))
            link(dve.tensor_copy(inw[0:W, :], stw[0:W, :]))

            dve.wait_ge(loaded["x"], 32)
            with dve.Fori(0, W) as i:
                dve.bn_stats(stats[:, :], xs[:, ds(i, 1), :].rearrange("p a c -> p (a c)")).then_inc(stat1, 1)
                dve.wait_ge(stat1, i + 1)
                pause()
                dve.bn_aggr(agg[:, :], stats[:, :]).then_inc(stat3, 1)
                dve.wait_ge(stat3, i + 1)
                dve.tensor_copy(mv[:, ds(i, 1), :].rearrange("p a c -> p (a c)"), agg[:, :]).then_inc(stat2, 1)
            dve.wait_ge(std_done, 1)
            dve.reciprocal(rs[:, :], sd[:, :]).then_inc(rstd_done, 1)
            dve.wait_ge(rstd_done, 1)
            link(dve.memset(tab[:, :, D:D + 1], 1.0))
            dve.wait_ge(loaded["weights"], 16 * 6)
            with dve.Fori(0, W) as i:
                dve.tensor_scalar(xn[:, :], xs[:, ds(i, 1), :].rearrange("p a c -> p (a c)"), mv[:, ds(i, 1), 0],
                                  rs[:, ds(i, 1)], ALU.subtract, ALU.mult).then_inc(n_xn, 1)
                row_i = tab[:, ds(i, 1), 0:D].rearrange("p a c -> p (a c)")
                dve.wait_ge(n_wh, i + 1)
                dve.tensor_tensor(row_i, bank[1][:, 0:D], wbb[:, :], ALU.add).then_inc(n_tab, 1)
                dve.wait_ge(n_tab, i + 1)
                dve.tensor_tensor(xn[:, :], row_i, adst[:, :], ALU.mult).then_inc(n_tab2, 1)
                dve.wait_ge(n_tab2, i * 2 + 1)
                dve.tensor_reduce(tab[:, ds(i, 1), D + 1], xn[:, :], AX.X, ALU.add).then_inc(n_fd, 1)
                dve.wait_ge(n_fd, i * 2 + 1)
                dve.tensor_tensor(xn[:, :], row_i, asrc[:, :], ALU.mult).then_inc(n_tab2, 1)
                dve.wait_ge(n_tab2, i * 2 + 2)
                dve.tensor_reduce(frc[:, ds(i, 1)], xn[:, :], AX.X, ALU.add).then_inc(n_fd, 1)
                dve.wait_ge(n_kraw, i + 1)
                dve.scalar_tensor_tensor(kk[:, :], ek[:, :], 1.0, rk[:, :], ALU.min, ALU.add).then_inc(n_kk, 1)
                dve.wait_ge(n_qraw, i + 1)
                dve.scalar_tensor_tensor(qT[:, :, ds(i * P, P)], eq[:, :].rearrange("p (h n) -> p h n", h=2), 1.0,
                                         rq[:, :].rearrange("p (h n) -> p h n", h=2), ALU.min, ALU.add
                                         ).then_inc(n_qT, 1)
                dve.wait_ge(n_fd, i * 2 + 2)

            dve.tensor_reduce(cmax[:, :], tab[:, :, D + 1], AX.X, ALU.max, apply_absolute_value=True
                              ).then_inc(c_in, 1)
            dve.wait_ge(c_ps, 1)
            dve.tensor_reduce(c1[:, :], bank[6][0:1, 0:P], AX.X, ALU.max).then_inc(c_in, 1)
            dve.wait_ge(c_ps, 2)
            link(dve.tensor_scalar(coff[:, :], bank[6][:, 0:1], 1.0, None, ALU.add))
            dve.wait_ge(c_ps, 3)
            dve.tensor_copy(frT[0:W, :], bank[7][0:W, 0:P]).then_inc(tiles_in, 1)
            link(dve.memset(bd[:, :, :], 0.0))
            dve.wait_ge(n_ctx, W)
            for hd in range(H):
                h, p = hd * DH // P, hd * DH % P
                dve.tensor_copy(bd[p:p + DH, h, hd * DH:(hd + 1) * DH], bank[4 + h][p:p + DH, hd * DH:(hd + 1) * DH])
                last = dve.tensor_copy(bd[p:p + DH, h, D + hd:D + hd + 1], bank[4 + h][p:p + DH, D:D + 1])
            last.then_inc(bd_done, 1)

            dve.wait_ge(table_out, 16)
            with dve.Fori(0, W) as i:
                x_i = xs[:, ds(i, 1), :].rearrange("p a c -> p (a c)")
                dve.wait_ge(a_num, i + 1)
                dve.tensor_scalar(dmx[:, :], bank[5][:, D:D + H], 1e-6, None, ALU.max).then_inc(a_dm, 1)
                dve.wait_ge(a_dm, i + 1)
                dve.reciprocal(dinv[:, :], dmx[:, :]).then_inc(a_di, 1)
                dve.wait_ge(a_di, i + 1)
                dve.tensor_tensor(att.rearrange("p (h d) -> p h d", h=H),
                                  bank[5][:, 0:D].rearrange("p (h d) -> p h d", h=H),
                                  dinv[:, :].rearrange("p (h a) -> p h a", a=1).to_broadcast([P, H, DH]), ALU.mult
                                  ).then_inc(a_att, 1)
                dve.wait_ge(a_pj, i + 1)
                dve.tensor_tensor(mixs, bank[7][:, 0:D], bpb[:, :], ALU.add).then_inc(a_mix, 1)
                dve.wait_ge(a_mix, i + 1)
                dve.tensor_tensor(x_i, x_i, mixs, ALU.add).then_inc(a_x, 1)
                dve.wait_ge(a_x, i + 1)

            for n in range(2):
                dve.wait_ge(loaded["experts"], 16 * (n + 1))
                dve.wait_ge(w_hi, n + 1)
                dve.tensor_tensor(wparts[2 * n + 1], stagew_e, wparts[2 * n], ALU.subtract).then_inc(w_lo, 1)
            dve.wait_ge(loaded["experts"], 16 * 4)
            link(dve.memset(b2p, 0.0))
            link(dve.tensor_copy(b2p[0:1, :], stageb[0:1, :]))
            link(dve.tensor_copy(b2p[32:33, :], stageb[32:33, :]))
            link(dve.tensor_tensor(b2p[32:33, :], stageb[32:33, :], b2p[32:33, :], ALU.subtract))
            dve.memset(onesh, 1.0).then_inc(b_parts, 1)

            last_group = dve.alloc_register("last_group")
            window = dve.alloc_register("window")
            dve.reg_mov(window, 0)
            dve.reg_load(last_group, tendi[0:1, 0:1])
            link(dve.memset(U, 0.0))
            link(dve.memset(mx[:, GR - 1:GR], 0.0))
            link(dve.memset(pr[:, GR - 1, 1:2], 0.0))
            dve.wait_ge(meta_sb, 2)

            def offset_values(g, r, k):
                dve.wait_ge(rows_in[r], k)
                dve.tensor_scalar(fdp[:, r, :], G[:, r, :, D + 1], coff[:, :], None, ALU.add).then_inc(e_fdp, 1)

            def one_hot(g, r, j):
                ins = dve.tensor_scalar(hot[:, r % 2, j, :], iotab[:, :], m4[:, r, j:j + 1], None, ALU.is_equal)
                if j == GT - 1:
                    ins.then_inc(e_hot, 1)

            def largest(g, r):
                dve.wait_ge(e_VT, g + 1)
                dve.tensor_reduce(mloc[:, r:r + 1], bank[turned[r % 2]][:, :], AX.X, ALU.max).then_inc(e_ml, 1)

            def running(g, r):
                dve.wait_ge(e_ml, g + 1)
                dve.scalar_tensor_tensor(mx[:, r:r + 1], mx[:, (r - 1) % GR:(r - 1) % GR + 1],
                                         m4[:, r, GT:GT + 1], mloc[:, r:r + 1], ALU.mult, ALU.max
                                         ).then_inc(e_mx, 1)

            def top_score(g, r):
                dve.wait_ge(e_mx, g + 1)
                dve.scalar_tensor_tensor(cc[:, r:r + 1], mx[:, r:r + 1], coff[:, :], pr[:, r, 0:1],
                                         ALU.subtract, ALU.add).then_inc(e_cc, 1)

            def shift(g, r):
                dve.wait_ge(e_cc, g + 1)
                dve.scalar_tensor_tensor(pr[:, r, 1:2], cc[:, r:r + 1], ALPHA, cc[:, r:r + 1], ALU.mult, ALU.max
                                         ).then_inc(e_R, 1)

            def shift_change(g, r):
                dve.wait_ge(e_R, g + 1)
                dve.tensor_scalar(gc[:, r:r + 1], pr[:, (r - 1) % GR, 1:2], pr[:, r, 1:2], 0.0, ALU.subtract, ALU.min
                                  ).then_inc(e_gc, 1)

            def scale(g, r):
                dve.wait_ge(e_ge, g + 1)
                dve.tensor_tensor(gg[:, r:r + 1], ge[:, r:r + 1], m4[:, r, GT:GT + 1], ALU.mult
                                  ).then_inc(e_gg, 1)

            def window_end(g):
                with dve.If(dve.snap(last_group) == g + 1):
                    w = dve.snap(window, min_val=0, max_val=W - 1)
                    dve.wait_ge(e_U, g + 1)
                    dve.tensor_scalar(dn[:, :], U[:, D:D + 1], 1e-30, None, ALU.max).then_inc(f_dn, 1)
                    dve.wait_ge(f_dn, w + 1)
                    dve.reciprocal(rd[:, :], dn[:, :]).then_inc(f_rd, 1)
                    dve.wait_ge(f_rd, w + 1)
                    dve.tensor_scalar(hh, U[:, 0:D], rd[:, :], 0.0, ALU.mult, ALU.max).then_inc(f_hh, 1)
                    dve.wait_ge(f_hh, w + 1)
                    x_w = xs[:, ds(w, 1), :].rearrange("p a c -> p (a c)")
                    dve.tensor_tensor(x_w, x_w, hh, ALU.add).then_inc(f_x, 1)
                    dve.wait_ge(f_x, w + 1)
                    pause()
                    dve.bn_stats(stats[:, :], x_w).then_inc(m_st, 1)
                    dve.wait_ge(m_st, w + 1)
                    pause()
                    dve.bn_aggr(agg[:, :], stats[:, :]).then_inc(m_ag0, 1)
                    dve.wait_ge(m_ag0, w + 1)
                    dve.tensor_copy(mv[:, ds(w, 1), :].rearrange("p a c -> p (a c)"), agg[:, :]).then_inc(m_ag, 1)
                    dve.wait_ge(m_ag, w + 1)
                    pause()
                    dve.reg_load(last_group, tendi[0:1, ds(w + 1, 1)])
                    dve.reg_add(window, window, 1)

            def add_up(g, r, first=False):
                if not first:
                    dve.wait_ge(e_U, g)
                dve.wait_ge(e_gg, g + 1)
                dve.wait_ge(e_A, g + 1)
                dve.scalar_tensor_tensor(U, U, gg[:, r:r + 1], bank[2 + r % 2][:, 0:D + 1], ALU.mult, ALU.add
                                         ).then_inc(e_U, 1)

            def step(g, r, k, first=False):
                n, nr, o, orr = g + 1, (r + 1) % GR, g + 2, (r + 2) % GR
                largest(n, nr)
                offset_values(o, orr, k)
                dve.wait_ge(e_m4, o + 1)
                if not (first and r < 0):
                    dve.wait_ge(e_Sa, o - 1)
                    dve.wait_ge(e_S, o - 1)
                running(n, nr)
                one_hot(o, orr, 0)
                top_score(n, nr)
                one_hot(o, orr, 1)
                shift(n, nr)
                one_hot(o, orr, 2)
                shift_change(n, nr)
                dve.wait_ge(e_fdp, o + 1)
                one_hot(o, orr, 3)
                ex_e = bank[1][:, 0:2 * GT].rearrange("p (j c) -> p j c", c=2)
                dve.wait_ge(e_EX, n + 1)
                dve.tensor_tensor(s1[:, nr, :], ex_e[:, :, 0], G[:, nr, :, D + 1], ALU.add).then_inc(e_s1, 1)
                if not (first and r < 1):
                    add_up(g - 1, (r - 1) % GR, first and r == 1)
                dve.wait_ge(e_s1, n + 1)
                dve.scalar_tensor_tensor(s2[:, nr, :], s1[:, nr, :], ALPHA, s1[:, nr, :], ALU.mult, ALU.max
                                         ).then_inc(e_s2, 1)
                scale(n, nr)
                dve.wait_ge(e_s2, n + 1)
                dve.tensor_tensor(s3[:, nr, :], s2[:, nr, :], ex_e[:, :, 1], ALU.subtract).then_inc(e_s3, 1)
                dve.wait_ge(e_s3, n + 1)
                dve.tensor_scalar(s4[:, nr, :], s3[:, nr, :], 0.0, None, ALU.min).then_inc(e_s4, 1)
                if not (first and r < 1):
                    window_end(g - 1)
                dve.wait_ge(e_w4, n + 1)
                if not (first and r < 1):
                    dve.wait_ge(e_A, n - 1)
                for j in range(SV):
                    ins = dve.tensor_scalar(S[:, nr % 2, j, :], hot[:, nr % 2, j, :], w4[:, nr, j:j + 1], None,
                                            ALU.mult)
                ins.then_inc(e_Sa, 1)

            offset_values(0, 0, 16 * GT)
            dve.wait_ge(e_m4, 1)
            dve.wait_ge(e_fdp, 1)
            for j in range(GT):
                one_hot(0, 0, j)
            step(-1, -1, 16 * GT, True)
            for r in range(GR):
                step(r, r, 16 * GT * (1 + (r + 2) // GR), True)
            with dve.Fori(1, NG // GR) as i:
                for r in range(GR):
                    step(i * GR + r, r, i * (16 * GT) + 16 * GT * (1 + (r + 2) // GR))
            add_up(NG - 1, GR - 1)
            window_end(NG - 1)

            dve.wait_ge(m_sd, 1)
            dve.reciprocal(rs[:, :], sd[:, :]).then_inc(m_rs, 1)
            dve.wait_ge(m_rs, 1)

            def norm(i):
                x_i = xs[:, ds(i, 1), :].rearrange("p a c -> p (a c)")
                dve.tensor_scalar(xn[:, :], x_i, mv[:, ds(i, 1), 0], rs[:, ds(i, 1)], ALU.subtract, ALU.mult
                                  ).then_inc(m_x2, 1)
                dve.wait_ge(m_x2, i + 1)
                dve.tensor_tensor(x_i, x_i, xn[:, :], ALU.add).then_inc(m_x1, 1)

            def norm_lo(i):
                cols = ds(i * P, P)
                dve.tensor_tensor(x2p[1][:, :, cols], xnT[:, :, :], x2p[0][:, :, cols], ALU.subtract
                                  ).then_inc(m_xlo, 1)

            dve.memset(started[:, 0:1], 0.0).then_inc(m_xlo, 1)
            norm(0)
            with dve.Fori(1, W) as i:
                dve.wait_ge(m_xt, i)
                dve.wait_ge(m_x1, i)
                norm(i)
                dve.wait_ge(m_xhi, i)
                norm_lo(i - 1)
            dve.wait_ge(m_xhi, W)
            norm_lo(W - 1)
            dve.memset(started[:, 1:2], 0.0).then_inc(m_lo, 1)
            dve.memset(started[:, 2:3], 0.0).then_inc(m_gelu, 4)
            dve.memset(started[:, 3:4], 0.0).then_inc(m_y, 2 * NB)
            dve.memset(started[:, 4:5], 0.0).then_inc(m_acc, NB)

            def wide(a):
                return a[:, :].rearrange("p (w a) -> p w a", a=1).to_broadcast([P, W, X])

            keys = from_end[:, :].rearrange("p (a e) -> p a e", a=1).to_broadcast([P, W, X])
            dve.wait_ge(m_lg, W)
            link(dve.tensor_copy(lg, bank[1][:, 0:W * X].rearrange("p (w e) -> p w e", e=X)))
            link(dve.tensor_reduce(top[:, :], lg, AX.X, ALU.max))
            dve.tensor_tensor(lg, lg, wide(top), ALU.subtract).then_inc(m_diff, 1)
            dve.wait_ge(m_diff, 1)

            def largest_of(v, one, value):
                link(dve.tensor_tensor(one, v, value, ALU.is_equal))
                link(dve.tensor_tensor(one, one, keys, ALU.mult))
                link(dve.tensor_reduce(key[:, :], one, AX.X, ALU.max))
                link(dve.tensor_tensor(one, keys, wide(key), ALU.is_equal))

            link(dve.memset(top[:, :], 0.0))
            largest_of(lg, one1, wide(top))
            link(dve.scalar_tensor_tensor(sc, one1, -3e38, lg, ALU.mult, ALU.add))
            link(dve.tensor_reduce(top[:, :], sc, AX.X, ALU.max))
            largest_of(sc, one2, wide(top))
            link(dve.tensor_tensor(one1, one1, one2, ALU.add))
            dve.wait_ge(m_ex, 1)
            link(dve.tensor_reduce(tot[:, :], ex, AX.X, ALU.add))
            link(dve.reciprocal(rt[:, :], tot[:, :]))
            link(dve.tensor_tensor(ex, ex, wide(rt), ALU.mult))
            link(dve.tensor_tensor(sc, ex, one1, ALU.mult))
            link(dve.tensor_reduce(tot[:, :], sc, AX.X, ALU.add))
            link(dve.tensor_scalar(tot[:, :], tot[:, :], 1e-12, None, ALU.max))
            link(dve.reciprocal(rt[:, :], tot[:, :]))
            link(dve.tensor_tensor(comb, sc, wide(rt), ALU.mult))

            def split(k, b, n):
                dve.wait_ge(m_hi, k + 1)
                dve.tensor_tensor(hTp[1][:, b, :, 0:n * P], hT[:, :, 0:n * P], hTp[0][:, b, :, 0:n * P],
                                  ALU.subtract).then_inc(m_lo, 1)

            def add(y, i, e, n):
                for j in range(n):
                    dve.wait_ge(m_y, y + (2 * NB + j + 1))
                    dve.wait_ge(m_acc, y + (NB - (n if e else NB) + j + 1))
                    x_w = xs[:, ds(i * NB + j, 1), :].rearrange("p a c -> p (a c)")
                    dve.scalar_tensor_tensor(x_w, bank[j][:, 0:D], comb[:, ds(i * NB + j, 1), e], x_w,
                                             ALU.mult, ALU.add).then_inc(m_acc, 1)

            def batch(i, n, after):
                for e in range(X):
                    if e + 1 < X:
                        split(i * X + (e + 1), (e + 1) % 2, n)
                    elif after:
                        split(i * X + (e + 1), (e + 1) % 2, after)
                    add(i * (NB * X) + n * e, i, e, n)

            dve.wait_ge(m_x1, W)
            split(0, 0, NB)
            with dve.Fori(0, FULL - 1) as i:
                batch(i, NB, NB)
            batch(FULL - 1, NB, REST)
            batch(FULL, REST, 0)


_INS = ['x', 'src', 'dst', 'L0_gnn_W_w', 'L0_gnn_W_b', 'L0_gnn_a_w', 'L0_gnn_a_b', 'L0_mix_Wq', 'L0_mix_Wkv',
        'L0_mix_Wproj', 'L0_mix_bproj', 'L0_ffn_router_w', 'L0_ffn_w1', 'L0_ffn_b1', 'L0_ffn_w2', 'L0_ffn_b2']


def kernel(**inputs):
    import numpy as _np
    import concourse.bacc as _bacc
    from concourse import mybir as _mybir
    from concourse.bass_utils import run_bass_kernel_spmd as _run

    nc = _bacc.Bacc("TRN2", target_bir_lowering=False, num_devices=1)
    arrays, args = {}, []
    for name in _INS:
        a = _np.ascontiguousarray(inputs[name])
        arrays[f"in_{name}_dram"] = a
        args.append(nc.dram_tensor(f"in_{name}_dram", a.shape, _mybir.dt.from_np(a.dtype), kind="ExternalInput").ap())
    shape = inputs['x'].shape
    args.append(nc.dram_tensor("out_dram", shape, _mybir.dt.float32, kind="ExternalOutput").ap())
    graph_layer(nc, *args)
    return _run(nc, [arrays], core_ids=[0]).results[0]["out_dram"]
```

```python
from contextlib import ExitStack

import concourse.bass as bass
from concourse import mybir

F32 = mybir.dt.float32
I32 = mybir.dt.int32
U16 = mybir.dt.uint16
BF16 = mybir.dt.bfloat16
F16 = mybir.dt.float16
ALU = mybir.AluOpType
ACT = mybir.ActivationFunctionType
AX = mybir.AxisListType

P = 128
ds = bass.ds


def graph_layer(nc, x, src, dst, W_w, W_b, a_w, a_b, Wq, Wkv, Wproj, bproj, router_w, w1, b1, w2, b2, out):
    N, D = x.shape
    E = src.shape[0]
    X = router_w.shape[0]
    H = 8
    DH = D // H
    ALPHA = 0.2
    W = -(-N // P)
    LAST = N - (W - 1) * P
    EC = -(-E // P)
    EFULL = E // EC
    EREST = E - EFULL * EC
    assert EFULL == P - 1 and EREST > 0
    FROM = P - 32
    GT = 4
    GE = GT * P
    GR = 6
    NG = (E + (GE - 1) * W + W - 1) // GE
    NGL = (NG - GR) // GR
    T = NG * GT
    TP = T + -(-EC // P)
    SC = 64
    SH = SC // 2
    CHUNKS = (SC, 3 * SC, EC)
    U7 = max(u for u in range(1, 8) if W % u == 0)
    TW = D + 2
    NB = 4
    FULL = (W - 1) // NB
    REST = W - FULL * NB

    table = nc.dram_tensor("table", [W * P, TW], F32).ap()
    binned = nc.dram_tensor("binned", [P * TP, 2], I32).ap()

    with ExitStack() as ctx:
        def sb(name, shape, dt=F32):
            return ctx.enter_context(nc.sbuf_tensor(name, shape, dt))

        def sem(name):
            return ctx.enter_context(nc.semaphore(name))

        xs = sb("xs", [P, W, D])
        work = sb("work", [P, W * TW])
        tab = work[:, :].rearrange("p (w c) -> p w c", w=W)
        tabh = work[:, :].bitcast(F16).rearrange("p (w c) -> p w c", w=W)
        place = [0]

        def part(*shape):
            n = 1
            for k in shape:
                n *= k
            a, place[0] = place[0], place[0] + n
            assert place[0] <= W * TW
            names = [f"d{k}" for k in range(len(shape))]
            v = work[:, a:a + n]
            if len(shape) > 1:
                v = v.rearrange(f"p ({' '.join(names)}) -> p {' '.join(names)}", **dict(zip(names, shape)))
            return v

        big = sb("big", [P, 2 * W * P])
        qT = big[:, :].rearrange("p (h n) -> p h n", h=2)
        WE = X * 2 * D
        wparts = [big[:, n * WE // 2:(n + 1) * WE // 2].bitcast(F16).rearrange("p (e h f) -> p e h f", e=X, h=2)
                  for n in range(4)]
        w1p, w2p = wparts[0:2], wparts[2:4]
        free = 2 * WE
        stagew = big[:, free:free + WE]
        stagew_e = stagew.rearrange("p (e h f) -> p e h f", e=X, h=2)
        stageb = big[0:33, free:free + X * D]
        hT = big[:, free:free + 2 * NB * P].rearrange("p (f n) -> p f n", f=2)
        free += 2 * NB * P
        hTp = []
        for n in range(2):
            hTp.append(big[:, free:free + 2 * NB * P].bitcast(F16).rearrange("p (b f n) -> p b f n", b=2, f=2))
            free += 2 * NB * P
        b2p = big[0:33, free:free + X * D // 2].bitcast(F16)
        onesh = big[0:33, free + X * D // 2:free + X * D // 2 + P // 2].bitcast(F16)
        assert free + X * D // 2 + P // 2 <= 2 * W * P
        wraw = big[:, 0:8 * D].rearrange("p (n c) -> p n c", n=8)
        b1r = big[0:X, 8 * D:9 * D]
        rws = big[0:X, 9 * D:10 * D]
        b1c = sb("b1c", [P, 2, X])
        rwT = sb("rwT", [P, 2, X])
        wws = sb("wws", [P, 2, D])
        wkvT = sb("wkvT", [P, 2, 2 * D])
        wqT = sb("wqT", [P, 2, D])
        wpT = sb("wpT", [P, 2, D])
        wbb = sb("wbb", [P, D])
        adst = sb("adst", [P, D])
        asrc = sb("asrc", [P, D])
        abb = sb("abb", [P, 1])
        bpb = sb("bpb", [P, D])
        ident = sb("ident", [P, P])
        onesf = sb("onesf", [P, P])
        before = sb("before", [P, P])
        iotap = sb("iotap", [P, P])
        iotab = sb("iotab", [P, P], F16)
        valid = sb("valid", [P, W])
        epsc = sb("epsc", [P, 1])
        srci = part(EC).bitcast(I32)
        dsti = part(EC).bitcast(I32)
        rank = part(2, EC)
        posf = part(EC)
        winb = part(EC // 2).bitcast(BF16)
        maskb = part(2, EC // 2).bitcast(BF16)
        onebf = part(EC // 2).bitcast(BF16)
        slot = sb("slot", [P, EC], I32)
        lst = sb("lst", [P, TP, 2], I32)
        rec = lst[:, 0:EC, :]
        lst_f = lst[:, :, :].rearrange("p t c -> p (t c)").bitcast(F32)
        cnt = sb("cnt", [P, W])
        ntf = sb("ntf", [P, W])
        nti = sb("nti", [P, W], I32)
        tend = sb("tend", [P, W])
        tendi = sb("tendi", [P, W + 1], I32)
        base = sb("base", [P, W])
        ntc = sb("ntc", [64, 1])
        ntci = sb("ntci", [64, 1], I32)
        tec = sb("tec", [64, 1])
        tsc = sb("tsc", [64, 1])
        sidx = sb("sidx", [P, 2, SH], I32)
        srec = sb("srec", [P, 2, SH, 2], I32)
        stats7 = sb("stats7", [P, U7, 6])
        agg7 = sb("agg7", [P, U7, 2])
        idle = sb("idle", [P, 1])
        rest = sb("rest", [P, 1])
        carry = sb("carry", [P, 1])
        mv = sb("mv", [P, W, 2])
        sd = sb("sd", [P, W])
        rs = sb("rs", [P, W])
        xn = sb("xn", [P, D])
        wh = sb("wh", [P, D])
        prod = sb("prod", [P, 2, D])
        xnT = sb("xnT", [P, 2, P])
        frc = sb("frc", [P, W])
        ek = sb("ek", [P, D])
        rk = sb("rk", [P, D])
        kk = sb("kk", [P, D])
        vv = sb("vv", [P, D + 1])
        eq = sb("eq", [P, D])
        rq = sb("rq", [P, D])
        cmax = sb("cmax", [P, 1])
        c1 = sb("c1", [1, 1])
        coff = sb("coff", [P, 1])
        frT = sb("frT", [64, P])
        inw = sb("inw", [64, NG])
        startw = sb("startw", [64, NG])
        stw = sb("stw", [64, NG])
        meta = sb("meta", [P, NG, GT + 3])
        bd = sb("bd", [P, 2, D + H])
        dinv = sb("dinv", [P, H])
        dmx = sb("dmx", [P, H])
        gidx = sb("gidx", [P, GR, GT], I32)
        place[0] = 0
        G = part(GR, GT, TW)
        Gh = work[:, 0:GR * GT * TW].bitcast(F16).rearrange("p (r j c) -> p r j c", r=GR, j=GT)
        hot = part(GR, GT, P // 2).bitcast(F16)
        V = part(2, GT, P)
        OT = part(2, GT, P)
        Sp = [part(2, GT, P // 2).bitcast(F16) for _ in range(2)]
        qs = part(2, P)
        att = part(D)
        attT = part(2, P)
        mixs = part(D)
        U = part(D + 1)
        hh = part(D)
        x2p = [work[:, n * W * P:(n + 1) * W * P].bitcast(F16).rearrange("p (h n) -> p h n", h=2) for n in range(2)]
        m4 = sb("m4", [P, GR, GT + 4])
        fdp = sb("fdp", [P, GR, GT])
        mloc = sb("mloc", [P, GR])
        mx = sb("mx", [P, GR])
        cc = sb("cc", [P, GR])
        pr = m4[:, :, GT + 2:GT + 4]
        gc = sb("gc", [P, GR])
        gg = sb("gg", [P, GR])
        s1 = sb("s1", [P, GR, GT])
        s2 = sb("s2", [P, GR, GT])
        s3 = sb("s3", [P, GR, GT])
        s4 = sb("s4", [P, GR, GT])
        w4 = sb("w4", [P, GR, GT])
        w4h = sb("w4h", [P, GR, GT], F16)
        w4l = sb("w4l", [P, GR, GT])
        dn = sb("dn", [P, 1])
        rd = sb("rd", [P, 1])
        x2 = (xn[:, :], wh[:, :])
        x2T = [xnT[:, :, :]] + [prod[:, n, :].rearrange("p (h c) -> p h c", h=2) for n in range(2)]
        norms = (0, 2, 3)
        lg, ex, sc, one1, one2 = (lst_f[:, n * W * X:(n + 1) * W * X].rearrange("p (w e) -> p w e", e=X)
                                  for n in range(5))
        comb = slot[:, 0:W * X].bitcast(F32).rearrange("p (w e) -> p w e", e=X)
        from_end = sb("from_end", [P, X])
        started = sb("started", [P, 6])
        none = sb("none", [P, 5])
        top, key, tot, rt = cnt, ntf, tend, base

        bank = [ctx.enter_context(nc.psum_tensor(f"bank{n}", [P, 512], F32)) for n in range(8)]

        loaded = {n: sem("loaded_" + n) for n in ("edges", "neighbours", "x", "raw", "weights", "experts", "list")}
        filled, padded = sem("filled"), sem("padded")
        consts = sem("consts")
        masks = sem("masks")
        blank = sem("blank")
        dv = sem("dv")
        counted, r_mask, r_scan, r_set = sem("counted"), sem("r_mask"), sem("r_scan"), sem("r_set")
        prefix, ntc_done, slot_done = sem("prefix"), sem("ntc_done"), sem("slot_done")
        staged = [sem(f"staged{i}") for i in range(2)]
        scattered = [sem(f"scattered{i}") for i in range(2)]
        wt_ps, wt_sb = sem("wt_ps"), sem("wt_sb")
        stat1, stat2, stat3, std_done, rstd_done = sem("stat1"), sem("stat2"), sem("stat3"), sem("std_done"), sem("rstd_done")
        n_xn, n_xt, n_xnT, n_wh, n_kv, n_q, n_tab, n_tab2, n_fd, n_hi, n_lo, n_kraw, n_kk, n_qraw, n_qT, n_ctx = (
            sem("n_" + k) for k in ("xn", "xt", "xnT", "wh", "kv", "q", "tab", "tab2", "fd", "hi", "lo", "kraw", "kk", "qraw", "qT",
                                    "ctx"))
        ctx_zero = sem("ctx_zero")
        table_out = sem("table_out")
        c_in, c_ps = sem("c_in"), sem("c_ps")
        tiles_in, meta_ps, meta_sb = sem("tiles_in"), sem("meta_ps"), sem("meta_sb")
        bd_done = sem("bd_done")
        a_qs, a_num, a_dm, a_di, a_att, a_at, a_attT, a_pj, a_mix, a_x = (
            sem("a_" + k) for k in ("qs", "num", "dm", "di", "att", "at", "attT", "pj", "mix", "x"))
        listed, carried = sem("listed"), sem("carried")
        rows_in = [sem(f"rows_in{i}") for i in range(GR)]
        (e_m4, e_fdp, e_hot, e_V, e_VT, e_ml, e_mx, e_cc, e_R, e_gc, e_gg, e_OT, e_EX, e_s1, e_s2,
         e_s3, e_s4, e_w4, e_w4l, e_Sl, e_S, e_A, e_U) = (sem("e_" + k) for k in (
             "m4", "fdp", "hot", "V", "VT", "ml", "mx", "cc", "R", "gc", "gg", "OT", "EX", "s1", "s2",
             "s3", "s4", "w4", "w4l", "Sl", "S", "A", "U"))
        f_dn, f_rd, f_hh, f_x = (sem("f_" + k) for k in ("dn", "rd", "hh", "x"))
        w_hi, w_lo, b_parts = sem("w_hi"), sem("w_lo"), sem("b_parts")
        m_st, m_ag0, m_ag, m_sd, m_rs, m_x2, m_x1, m_xt, m_xhi, m_xlo, m_lg, m_diff, m_ex = (
            sem("m_" + k) for k in ("st", "ag0", "ag", "sd", "rs", "x2", "x1", "xt", "xhi", "xlo", "lg", "diff", "ex"))
        m_up, m_gelu, m_hi, m_lo, m_y, m_acc, m_out = (
            sem("m_" + k) for k in ("up", "gelu", "hi", "lo", "y", "acc", "out"))

        binned_p = binned.rearrange("(p t) c -> p t c", t=TP)
        assert NG <= 512
        turned, spreads, sums = (0, 6), (1, 7), (2, 3)

        def row(a, n):
            return a.rearrange("(a n) -> a n", a=1).to_broadcast([n, a.shape[0]])

        block = ctx.enter_context(nc.Block())

        @block.sync
        def _(sp):
            a = FROM
            for n, (arr, buf) in enumerate(((src, srci), (dst, dsti))):
                edges = loaded["edges" if n == 0 else "neighbours"]
                sp.dma_start(buf[0:a, :], arr[0:a * EC].rearrange("(p c) -> p c", c=EC)).then_inc(edges, 16)
                sp.wait_ge(padded, 2)
                sp.dma_start(buf[a:EFULL, :], arr[a * EC:EFULL * EC].rearrange("(p c) -> p c", c=EC)
                             ).then_inc(edges, 16)
                sp.dma_start(buf[EFULL:EFULL + 1, 0:EREST], arr[EFULL * EC:E].rearrange("(p c) -> p c", p=1)
                             ).then_inc(edges, 16)
            sp.wait_ge(filled, 1)
            sp.dma_start(xs[:, 0:W - 1, :], x[0:(W - 1) * P, :].rearrange("(w p) c -> p w c", p=P)
                         ).then_inc(loaded["x"], 16)
            sp.dma_start(xs[0:LAST, W - 1, :], x[(W - 1) * P:N, :]).then_inc(loaded["x"], 16)
            sp.wait_ge(filled, 3)
            sp.dma_start(binned_p, lst[:, :, :]).then_inc(blank, 16)
            sp.dma_start(wraw[:, 0:2, :], Wq.rearrange("(h p) c -> p h c", p=P)).then_inc(loaded["raw"], 16)
            sp.dma_start(wraw[:, 2:6, :], Wkv.rearrange("(h p) c -> p h c", p=P)).then_inc(loaded["raw"], 16)
            sp.dma_start(wraw[:, 6:8, :], Wproj.rearrange("(h p) c -> p h c", p=P)).then_inc(loaded["raw"], 16)
            sp.dma_start(rws, router_w).then_inc(loaded["raw"], 16)
            sp.dma_start(b1r, b1).then_inc(loaded["raw"], 16)
            sp.dma_start(wws[:, :, :], W_w.rearrange("(h p) c -> p h c", p=P)).then_inc(loaded["weights"], 16)
            sp.dma_start(wbb[:, :], row(W_b, P)).then_inc(loaded["weights"], 16)
            sp.dma_start(adst[:, :], row(a_w[0:D], P)).then_inc(loaded["weights"], 16)
            sp.dma_start(asrc[:, :], row(a_w[D:2 * D], P)).then_inc(loaded["weights"], 16)
            sp.dma_start(abb[:, :], row(a_b, P)).then_inc(loaded["weights"], 16)
            sp.dma_start(bpb[:, :], row(bproj, P)).then_inc(loaded["weights"], 16)
            sp.wait_ge(n_fd, 2 * W)
            sp.wait_ge(n_hi, W)
            sp.wait_ge(n_lo, W)
            sp.dma_start(table.rearrange("(w p) c -> p w c", p=P), tab[:, :, :]).then_inc(table_out, 16)
            sp.wait_ge(a_qs, W)
            sp.dma_start(stagew_e, w1.rearrange("e (h p) f -> p e h f", p=P)).then_inc(loaded["experts"], 16)
            sp.wait_ge(w_hi, 1)
            sp.wait_ge(w_lo, 1)
            sp.dma_start(stagew_e, w2.rearrange("e (h p) f -> p e h f", p=P)).then_inc(loaded["experts"], 16)
            sp.wait_ge(w_hi, 2)
            sp.wait_ge(w_lo, 2)
            for n in (0, 32):
                sp.dma_start(stageb[n:n + 1, :], b2.rearrange("(a e) d -> a (e d)", a=1)
                             ).then_inc(loaded["experts"], 16)
            sp.wait_ge(scattered[0], 16 * (SH * (EC // SC) + min(SH, EC % SC)))
            sp.wait_ge(scattered[1], 16 * (SH * (EC // SC) + max(0, EC % SC - SH)))
            sp.dma_start(lst[:, :, :], binned_p).then_inc(loaded["list"], 16)
            def result(i, n):
                rows = ds(i * (NB * P), n * P)
                sp.dma_start(out[rows, :].rearrange("(w p) c -> p w c", p=P), xs[:, ds(i * NB, n), :]
                             ).then_inc(m_out, 16)

            with sp.Fori(0, FULL) as i:
                sp.wait_ge(m_acc, i * (NB * X) + (NB * X + NB))
                result(i, NB)
            sp.wait_ge(m_acc, FULL * NB * X + REST * X + NB)
            if REST > 1:
                result(FULL, REST - 1)
            sp.dma_start(out[(W - 1) * P:N, :], xs[0:LAST, W - 1, :]).then_inc(m_out, 16)
            sp.wait_ge(m_out, 16 * (FULL + min(REST, 2)))

        @block.gpsimd
        def _(pool):
            pool.memset(xs[:, W - 1, :], 0.0).then_inc(filled, 1)
            pool.memset(lst[:, :, 0], 0).then_inc(filled, 1)
            pool.memset(lst[:, :, 1], -1).then_inc(filled, 1)
            pool.iota(posf, pattern=[[1, EC]], base=T * P, channel_multiplier=0,
                      allow_small_or_imprecise_dtypes=True).then_inc(consts, 1)
            pool.iota(iotap[:, :], pattern=[[1, P]], base=0, channel_multiplier=0,
                      allow_small_or_imprecise_dtypes=True).then_inc(consts, 1)
            pool.iota(iotab[:, :], pattern=[[1, P]], base=0, channel_multiplier=0,
                      allow_small_or_imprecise_dtypes=True).then_inc(consts, 1)
            pool.memset(onesf[:, :], 1.0).then_inc(consts, 1)
            pool.memset(onebf, 1.0).then_inc(consts, 1)
            pool.memset(before[:, :], 1.0).then_inc(masks, 1)
            pool.memset(ident[:, :], 0.0).then_inc(masks, 1)
            pool.memset(valid[:, :], 1.0).then_inc(masks, 1)
            pool.wait_ge(masks, 3)
            pool.affine_select(out=before[:, :], in_=before[:, :], compare_op=ALU.is_gt, fill=0.0, base=0,
                               pattern=[[1, P]], channel_multiplier=-1).then_inc(consts, 1)
            pool.affine_select(out=ident[:, :], in_=ident[:, :], compare_op=ALU.not_equal, fill=1.0, base=0,
                               pattern=[[-1, P]], channel_multiplier=1).then_inc(consts, 1)
            pool.affine_select(out=valid[:, W - 1:W], in_=valid[:, W - 1:W], compare_op=ALU.is_gt, fill=0.0,
                               base=LAST, pattern=[[0, 1]], channel_multiplier=-1).then_inc(consts, 1)
            pool.memset(kk[:, 0:P], 0.0).then_inc(consts, 1)
            pool.memset(epsc[:, :], 1e-5).then_inc(consts, 1)
            pool.iota(inw[:, :], pattern=[[1, NG]], base=0, channel_multiplier=0,
                      allow_small_or_imprecise_dtypes=True).then_inc(consts, 1)

            pool.iota(from_end[:, :], pattern=[[-1, X]], base=X, channel_multiplier=0,
                      allow_small_or_imprecise_dtypes=True).then_inc(consts, 1)

            pool.wait_ge(slot_done, 1)
            pool.wait_ge(blank, 16)

            def stage(c, n, b):
                pool.tensor_copy(sidx[:, b, 0:n], slot[:, c]).then_inc(staged[b], 1)
                pool.tensor_copy(srec[:, b, 0:n, :], rec[:, c, :]).then_inc(staged[b], 1)

            def scatter(b, n):
                pool.tensor_tensor(rest[:, :], iotap[:, 0:1], iotap[:, 0:1], ALU.add)
                for j in range(n):
                    pool.indirect_dma_start(binned, bass.IndirectOffsetOnAxis(ap=sidx[:, b, j:j + 1], axis=0),
                                            srec[:, b, j, :], None).then_inc(scattered[b], 16)

            for b in range(2):
                stage(slice(b * SH, (b + 1) * SH), SH, b)
                pool.wait_ge(staged[b], 2)
                scatter(b, SH)
            full = EC // SC
            for q, to in enumerate(CHUNKS[1:]):
                pool.wait_ge(slot_done, q + 2)
                with pool.Fori(CHUNKS[q] // SC, to // SC) as i:
                    for b in range(2):
                        pool.wait_ge(scattered[b], i * (16 * SH))
                        stage(ds(i * SC + b * SH, SH), SH, b)
                        pool.wait_ge(staged[b], i * 2 + 2)
                        scatter(b, SH)
            for b in range(2):
                n = min(SH, EC - full * SC - b * SH)
                if n > 0:
                    pool.wait_ge(scattered[b], full * 16 * SH)
                    stage(slice(full * SC + b * SH, full * SC + b * SH + n), n, b)
                    pool.wait_ge(staged[b], full * 2 + 2)
                    scatter(b, n)

            pool.wait_ge(loaded["list"], 16)
            pool.wait_ge(table_out, 16)
            pool.wait_ge(c_in, 1)

            def gather(g, r):
                if not (isinstance(g, int) and g == 0):
                    pool.wait_ge(carried, g)
                pool.wait_ge(listed, g + 1)
                pool.tensor_tensor(carry[:, :], iotap[:, 0:1], iotap[:, 0:1], ALU.add).then_inc(carried, 1)
                for j in range(GT):
                    pool.indirect_dma_start(G[:, r, j, :], None, table,
                                            bass.IndirectOffsetOnAxis(ap=gidx[:, r, j:j + 1], axis=0)
                                            ).then_inc(rows_in[r], 16)

            pool.wait_ge(a_x, W)
            for r in range(GR):
                gather(r, r)
            with pool.Fori(1, NGL) as i:
                for r in range(GR):
                    pool.wait_ge(e_A, i * GR + (r + 1 - GR))
                    gather(i * GR + r, r)
            for g in range(NGL * GR, NG):
                pool.wait_ge(e_A, g + 1 - GR)
                gather(g, g % GR)

        @block.scalar
        def _(act):
            for n, o in enumerate((wqT[:, :, 0:P], wqT[:, :, P:D], wkvT[:, :, 0:P], wkvT[:, :, P:2 * P],
                                   wkvT[:, :, 2 * P:3 * P], wkvT[:, :, 3 * P:4 * P], wpT[:, :, 0:P],
                                   wpT[:, :, P:D])):
                act.wait_ge(wt_ps, n + 1)
                act.copy(o, bank[n][:, 0:D].rearrange("p (h c) -> p h c", h=2)).then_inc(wt_sb, 1)
            act.wait_ge(wt_ps, 9)
            act.copy(rwT[:, :, :], bank[0][:, 0:2 * X].rearrange("p (h c) -> p h c", h=2)).then_inc(wt_sb, 1)
            act.copy(b1c[:, :, :], bank[0][:, 2 * X:4 * X].rearrange("p (h e) -> p h e", h=2)).then_inc(wt_sb, 1)
            act.wait_ge(consts, 12)
            act.wait_ge(stat2, W // U7)
            act.activation(sd[:, :], mv[:, :, 1], ACT.Sqrt, bias=epsc[:, :]).then_inc(std_done, 1)

            def turned_norm(i):
                act.wait_ge(n_xt, i + 1)
                act.copy(xnT[:, :, :], bank[0][:, 0:D].rearrange("p (h c) -> p h c", h=2)).then_inc(n_xnT, 1)

            def node(i, more=True):
                act.wait_ge(n_kv, i + 1)
                act.activation(ek[:, :], bank[2][:, 0:D], ACT.Exp)
                act.activation(rk[:, :], bank[2][:, 0:D], ACT.Relu)
                act.copy(vv[:, 0:D], bank[2][:, D:2 * D])
                act.copy(vv[:, D:D + 1], valid[:, ds(i, 1)]).then_inc(n_kraw, 1)
                act.wait_ge(n_q, i + 1)
                act.activation(eq[:, :], bank[3][:, 0:D], ACT.Exp)
                act.activation(rq[:, :], bank[3][:, 0:D], ACT.Relu).then_inc(n_qraw, 1)
                if more:
                    turned_norm(i + 1)
                act.wait_ge(n_tab, i + 1)
                act.copy(tabh[:, ds(i, 1), 0:D].rearrange("p a c -> p (a c)"), wh[:, :]).then_inc(n_hi, 1)

            act.activation(started[:, 4:5], epsc[:, :], ACT.Exp)
            turned_norm(0)
            with act.Fori(0, W - 1) as i:
                node(i)
            node(W - 1, False)

            act.wait_ge(meta_ps, 1)
            act.activation(meta[:, :, GT + 1], bank[1][:, 0:NG], ACT.Copy, scale=-1e30)
            act.activation(meta[:, :, GT + 2], bank[0][:, 0:NG], ACT.Identity, bias=abb[:, :])
            act.activation(meta[:, :, GT], bank[1][:, 0:NG], ACT.Copy, bias=1.0, scale=-1.0
                           ).then_inc(meta_sb, 1)

            act.wait_ge(table_out, 16)
            act.wait_ge(bd_done, 1)
            def queries(i, waits=True):
                if waits:
                    act.wait_ge(a_num, i)
                act.copy(qs[:, :, :], qT[:, :, ds(i * P, P)]).then_inc(a_qs, 1)

            def attended(i):
                act.wait_ge(a_at, i + 1)
                act.copy(attT[:, :, :], bank[6][:, 0:D].rearrange("p (h c) -> p h c", h=2)).then_inc(a_attT, 1)

            queries(0, False)
            with act.Fori(0, W - 1) as i:
                queries(i + 1)
                attended(i)
            attended(W - 1)

            for n in range(2):
                act.wait_ge(loaded["experts"], 16 * (n + 1))
                act.copy(wparts[2 * n], stagew_e).then_inc(w_hi, 1)

            act.wait_ge(loaded["list"], 16)
            act.copy(meta[:, :, 0:GT], lst[:, 0:NG * GT, 1].rearrange("p (g j) -> p g j", j=GT)).then_inc(meta_sb, 1)
            act.wait_ge(meta_sb, 2)

            def group_data(g, r, c):
                act.copy(m4[:, r, 0:GT + 3], meta[:, c, :]).then_inc(e_m4, 1)

            def one_hot_turned(g):
                act.wait_ge(e_ml, g[0] + 1)
                b = g[1] % 2
                act.activation(OT[:, b, :, :], bank[turned[b]][:, :].rearrange("p (j e) -> p j e", j=GT), ACT.Sign
                               ).then_inc(e_OT, 1)

            def values(g, k):
                r = g[1] % GR
                act.wait_ge(rows_in[r], k)
                act.activation(fdp[:, r, :], G[:, r, :, D + 1], ACT.Identity, bias=coff[:, :]).then_inc(e_fdp, 1)
                act.wait_ge(e_hot, g[0] + 1)
                act.wait_ge(e_fdp, g[0] + 1)
                for j in range(GT):
                    ins = act.activation(V[:, r % 2, j, :], hot[:, r, j, :], ACT.Copy, scale=fdp[:, r, j:j + 1])
                ins.then_inc(e_V, 1)

            def exps(g):
                r = g[1] % GR
                act.wait_ge(e_s4, g[0] + 1)
                act.activation(w4[:, r, :], s4[:, r, :], ACT.Exp)
                act.activation(w4h[:, r, :], s4[:, r, :], ACT.Exp).then_inc(e_w4, 1)

            def weights(g, freed=True):
                r = g[1] % GR
                act.wait_ge(e_w4, g[0] + 1)
                if freed:
                    act.wait_ge(e_A, g[0] - 1)
                for j in range(GT):
                    ins = act.activation(Sp[0][:, r % 2, j, :], hot[:, r, j, :], ACT.Copy,
                                         scale=w4[:, r, j:j + 1])
                ins.then_inc(e_S, 1)

            def change(g):
                r = g[1] % GR
                act.wait_ge(e_gc, g[0] + 1)
                act.activation(gg[:, r:r + 1], gc[:, r:r + 1], ACT.Exp, bias=m4[:, r, GT + 1:GT + 2]
                               ).then_inc(e_gg, 1)

            def neighbours(r, c):
                act.copy(gidx[:, r, :], lst[:, c, 0]).then_inc(listed, 1)

            def step(g, r, k, first=False, left=NG):
                if left > 3:
                    values((g + 3, r + 3), k)
                if left > 2:
                    one_hot_turned((g + 2, r + 2))
                if not (first and r < -1) and left > 1:
                    exps((g + 1, r + 1))
                if left > 2:
                    change((g + 2, r + 2))
                if not (first and r < 0):
                    if left > GR:
                        neighbours(r, slice((g + GR) * GT, (g + GR + 1) * GT) if first or left < NG else
                                   ds(g * GT + GR * GT, GT))
                    if left > 4:
                        group_data(g + 4, (r + 4) % GR, slice(g + 4, g + 5) if first or left < NG else ds(g + 4, 1))
                if not (first and r < -1) and left > 1:
                    weights((g + 1, r + 1), not (first and r < 1))

            for r in range(GR):
                neighbours(r, slice(r * GT, (r + 1) * GT))
            for g in range(4):
                group_data(g, g, slice(g, g + 1))
            values((0, 0), 16 * GT)
            for r in range(-2, GR):
                step(r, r, 16 * GT * (1 + (r + 3) // GR), True)
            with act.Fori(1, NGL) as i:
                for r in range(GR):
                    step(i * GR + r, r, i * (16 * GT) + 16 * GT * (1 + (r + 3) // GR))
            for g in range(NGL * GR, NG):
                step(g, g % GR, 16 * GT * (1 + (g + 3) // GR), left=NG - g)

            act.wait_ge(m_ag, W // U7)
            act.activation(sd[:, :], mv[:, :, 1], ACT.Sqrt, bias=epsc[:, :]).then_inc(m_sd, 1)
            with act.Fori(0, W // U7) as i:
                for u in range(U7):
                    w = i * U7 + u
                    act.wait_ge(m_xt, w + 2)
                    if u == 0 or u > 2:
                        act.wait_ge(m_xlo, w + (-1 if u else 1))
                        act.wait_ge(m_lg, w + (-1 if u else 1))
                    x2t = bank[norms[u % 3]][:, 0:D].rearrange("p (h c) -> p h c", h=2)
                    act.copy(x2p[0][:, :, ds(w * P, P)], x2t)
                    act.copy(x2T[u % 3], x2t).then_inc(m_xhi, 1)
            act.wait_ge(m_diff, 1)
            act.activation(ex, lg, ACT.Exp).then_inc(m_ex, 1)
            act.wait_ge(b_parts, 1)

            def hidden(k, b, e, n):
                act.wait_ge(m_up, k + 1)
                act.wait_ge(m_lo, k + 1)
                for f in range(2):
                    act.activation(hT[:, f, 0:n * P], bank[4 + 2 * b + f][:, 0:n * P], ACT.Gelu,
                                   bias=b1c[:, f, e:e + 1]).then_inc(m_gelu, 1)
                act.wait_ge(m_gelu, k * 2 + 6)
                act.copy(hTp[0][:, b, :, 0:n * P], hT[:, :, 0:n * P]).then_inc(m_hi, 1)

            with act.Fori(0, FULL) as i:
                for e in range(X):
                    act.wait_ge(m_y, i * (NB * X) + (NB * e + NB))
                    hidden(i * X + e, e % 2, e, NB)
            for e in range(X):
                act.wait_ge(m_y, 2 * NB + FULL * NB * X + (REST * (e - 1) if e else -NB))
                hidden(FULL * X + e, e % 2, e, REST)

        @block.tensor
        def _(pe):
            pe.wait_ge(consts, 12)
            pe.wait_ge(loaded["raw"], 16 * 5)
            for n in range(8):
                for h in range(2):
                    mm = pe.transpose(bank[n][:, h * P:(h + 1) * P], wraw[:, n, h * P:(h + 1) * P], ident[:, :])
                mm.then_inc(wt_ps, 1)
            pe.wait_ge(wt_sb, 1)
            for h in range(2):
                pe.transpose(bank[0][:, h * X:(h + 1) * X], rws[:, h * P:(h + 1) * P], ident[0:X, 0:X])
                mm = pe.transpose(bank[0][:, (2 + h) * X:(3 + h) * X], b1r[:, h * P:(h + 1) * P], ident[0:X, 0:X])
            mm.then_inc(wt_ps, 1)
            pe.wait_ge(wt_sb, 10)
            pe.wait_ge(counted, W)
            pe.matmul(bank[7][:, 0:W], before[:, :], cnt[:, :], start=True, stop=True)
            pe.matmul(bank[7][:, 64:64 + W], onesf[:, :], cnt[:, :], start=True, stop=True)
            pe.matmul(bank[7][0:W, 128:129], cnt[:, :], onesf[:, 0:1], start=True, stop=True).then_inc(prefix, 1)
            pe.wait_ge(ntc_done, 1)
            pe.matmul(bank[6][0:W, 0:1], before[0:W, 0:W], ntc[0:W, :], start=True, stop=True).then_inc(prefix, 1)

            pe.wait_ge(loaded["weights"], 16 * 6)
            for h in range(2):
                pe.matmul(bank[4 + h][:, 0:D + 1], kk[:, 0:P], wkvT[:, 0, 0:D + 1], start=True, stop=True)
            def turn_norm(i):
                pe.wait_ge(n_xn, i + 1)
                for h in range(2):
                    mm = pe.transpose(bank[0][:, h * P:(h + 1) * P], xn[:, h * P:(h + 1) * P], ident[:, :])
                mm.then_inc(n_xt, 1)

            def node(i, more=True):
                pe.wait_ge(n_xnT, i + 1)
                for h in range(2):
                    mm = pe.matmul(bank[1][:, 0:D], xnT[:, h, :], wws[:, h, :], start=(h == 0), stop=(h == 1))
                mm.then_inc(n_wh, 1)
                for h in range(2):
                    mm = pe.matmul(bank[2][:, :], xnT[:, h, :], wkvT[:, h, :], start=(h == 0), stop=(h == 1))
                mm.then_inc(n_kv, 1)
                for o in range(2):
                    for h in range(2):
                        mm = pe.matmul(bank[3][:, o * P:(o + 1) * P], wqT[:, h, o * P:(o + 1) * P], xnT[:, h, :],
                                       start=(h == 0), stop=(h == 1))
                mm.then_inc(n_q, 1)
                if more:
                    turn_norm(i + 1)
                pe.wait_ge(n_kk, i + 1)
                pe.wait_ge(n_qT, i + 1)
                for h in range(2):
                    mm = pe.matmul(bank[4 + h][:, 0:D + 1], kk[:, h * P:(h + 1) * P], vv[:, :], start=False,
                                   stop=True, skip_group_check=True)
                mm.then_inc(n_ctx, 1)

            turn_norm(0)
            with pe.Fori(0, W - 1) as i:
                node(i)
            node(W - 1, False)

            pe.wait_ge(c_in, 1)
            pe.transpose(bank[6][0:1, 0:P], cmax[:, :], ident[:, :]).then_inc(c_ps, 1)
            pe.wait_ge(c_in, 2)
            pe.matmul(bank[6][:, 0:1], onesf[0:1, :], c1[:, :], start=True, stop=True).then_inc(c_ps, 1)
            pe.transpose(bank[7][0:W, 0:P], frc[:, :], ident[:, :]).then_inc(c_ps, 1)
            pe.wait_ge(tiles_in, 1)
            pe.matmul(bank[0][:, 0:NG], frT[0:W, :], inw[0:W, :], start=True, stop=True)
            pe.matmul(bank[1][:, 0:NG], onesf[0:W, :], startw[0:W, :], start=True, stop=True).then_inc(meta_ps, 1)

            pe.wait_ge(bd_done, 1)
            pe.wait_ge(meta_sb, 1)
            def numerators(i):
                pe.wait_ge(a_qs, i + 1)
                for h in range(2):
                    mm = pe.matmul(bank[5][:, 0:D + H], qs[:, h, :], bd[:, h, :], start=(h == 0), stop=(h == 1))
                mm.then_inc(a_num, 1)

            def project(i, more=True):
                pe.wait_ge(a_att, i + 1)
                for h in range(2):
                    mm = pe.transpose(bank[6][:, h * P:(h + 1) * P], att[:, h * P:(h + 1) * P], ident[:, :])
                mm.then_inc(a_at, 1)
                if more:
                    numerators(i + 1)
                pe.wait_ge(a_attT, i + 1)
                for h in range(2):
                    mm = pe.matmul(bank[7][:, 0:D], attT[:, h, :], wpT[:, h, :], start=(h == 0), stop=(h == 1))
                mm.then_inc(a_pj, 1)

            numerators(0)
            project(0)
            with pe.Fori(1, W - 1) as i:
                pe.wait_ge(a_mix, i)
                project(i)
            pe.wait_ge(a_mix, W - 1)
            project(W - 1, False)
            pe.wait_ge(a_mix, W)

            def turn(g, r):
                b = r % 2
                pe.wait_ge(e_V, g + 1)
                for j in range(GT):
                    mm = pe.transpose(bank[turned[b]][:, j * P:(j + 1) * P], V[:, b, j, :], ident[:, :])
                mm.then_inc(e_VT, 1)

            def spread(g, r):
                pe.wait_ge(e_OT, g + 1)
                pe.wait_ge(e_R, g + 1)
                pe.wait_ge(e_m4, g + 1)
                for j in range(GT):
                    mm = pe.matmul(bank[spreads[r % 2]][:, 2 * j:2 * j + 2], OT[:, r % 2, j, :], pr[:, r % GR, :],
                                   start=True, stop=True)
                mm.then_inc(e_EX, 1)

            def total(g, r, first):
                pe.wait_ge(e_S, g + 1)
                pe.wait_ge(e_Sl, g + 1)
                if not (first and r < 2):
                    pe.wait_ge(e_U, g - 1)
                b = r % 2
                for j in range(GT):
                    pe.matmul(bank[sums[b]][:, 0:D + 1], Sp[0][:, b, j, :], Gh[:, r, j, 0:D + 1],
                              start=(j == 0), stop=False)
                    pe.matmul(bank[sums[b]][:, 0:D], Sp[0][:, b, j, :], Gh[:, r, j, D + 2:2 * D + 2],
                              start=False, stop=False)
                    mm = pe.matmul(bank[sums[b]][:, 0:D + 1], Sp[1][:, b, j, :], Gh[:, r, j, 0:D + 1],
                                   start=False, stop=(j == GT - 1))
                mm.then_inc(e_A, 1)

            def step(g, r, first=False, left=NG):
                if not (first and r < 0):
                    total(g, r, first)
                if left > 3:
                    turn(g + 3, r + 3)
                if left > 2:
                    spread(g + 2, r + 2)

            pe.wait_ge(table_out, 16)
            turn(0, 0)
            for r in range(-2, GR):
                step(r, r, True)
            with pe.Fori(1, NGL) as i:
                for r in range(GR):
                    step(i * GR + r, r)
            for g in range(NGL * GR, NG):
                step(g, g % GR, left=NG - g)

            with pe.Fori(0, W // U7) as i:
                for u in range(U7 + 1):
                    w = i * U7 + u
                    if u < U7:
                        pe.wait_ge(m_x2, w + 1)
                        pe.wait_ge(m_xhi, w + (-1 if u > 2 else 1))
                        for h in range(2):
                            mm = pe.transpose(bank[norms[u % 3]][:, h * P:(h + 1) * P],
                                              x2[u % 2][:, h * P:(h + 1) * P], ident[:, :])
                        mm.then_inc(m_xt, 1)
                    if u:
                        pe.wait_ge(m_xhi, w + 1)
                        for h in range(2):
                            mm = pe.matmul(bank[1][:, ds((w - 1) * X, X)], x2T[(u - 1) % 3][:, h, :], rwT[:, h, :],
                                           start=(h == 0), stop=(h == 1))
                        mm.then_inc(m_lg, 1)

            PAIRS = ((0, 0), (0, 1), (1, 0))

            def up(k, b, e, i, n):
                pe.wait_ge(m_gelu, k * 2 + 2)
                for f in range(2):
                    for h in range(2):
                        for m, (pw, px) in enumerate(PAIRS):
                            mm = pe.matmul(bank[4 + 2 * b + f][:, 0:n * P], w1p[pw][:, e, h, f * P:(f + 1) * P],
                                           x2p[px][:, h, ds(i * (NB * P), n * P)], start=(h + m == 0),
                                           stop=(h == 1 and m == 2))
                mm.then_inc(m_up, 1)

            def down(k, y, b, e, n):
                pe.wait_ge(m_lo, k + 2)
                for j in range(n):
                    pe.wait_ge(m_acc, y + (NB - (n if e else NB) + j + 1))
                    pe.matmul(bank[j][:, 0:D], onesh, b2p[:, e * D:(e + 1) * D], start=True, stop=False)
                    for f in range(2):
                        for m, (ph, pw) in enumerate(PAIRS):
                            mm = pe.matmul(bank[j][:, 0:D], hTp[ph][:, b, f, j * P:(j + 1) * P], w2p[pw][:, e, f, :],
                                           start=False, stop=(f == 1 and m == 2))
                    mm.then_inc(m_y, 1)

            def batch(i, n, after):
                for e in range(X):
                    if e + 1 < X:
                        up(i * X + (e + 1), (e + 1) % 2, e + 1, i, n)
                    elif after:
                        up(i * X + (e + 1), (e + 1) % 2, 0, i + 1, after)
                    down(i * X + e, i * (NB * X) + n * e, e % 2, e, n)

            pe.wait_ge(b_parts, 1)
            pe.wait_ge(m_xlo, W + 1)
            up(0, 0, 0, 0, NB)
            with pe.Fori(0, FULL - 1) as i:
                batch(i, NB, NB)
            batch(FULL - 1, NB, REST)
            batch(FULL, REST, 0)

        @block.vector
        def _(dve):
            steps = [0]

            def link(ins):
                steps[0] += 1
                ins.then_inc(dv, 1)
                dve.wait_ge(dv, steps[0])

            def pause():
                dve.memset(idle[:, :], 0.0)

            dve.memset(srci[FROM:P, EREST:EC], (W + 1) * P).then_inc(padded, 1)
            dve.memset(dsti[FROM:P, EREST:EC], 0).then_inc(padded, 1)
            dve.wait_ge(loaded["edges"], 16 * 3)
            dve.wait_ge(consts, 5)
            link(dve.tensor_scalar(slot[:, :], srci, 7, None, ALU.logical_shift_right))
            link(dve.tensor_copy(winb, slot[:, :]))
            with dve.Fori(0, W // U7) as i:
                for u in range(U7):
                    if u > 1:
                        dve.wait_ge(counted, i * U7 + (u - 1))
                    dve.tensor_scalar(maskb[:, u % 2, :], winb, iotap[:, ds(i * U7 + u, 1)], None, ALU.is_equal, ALU.add,
                                      accum_out=cnt[:, ds(i * U7 + u, 1)]).then_inc(counted, 1)
                dve.wait_ge(counted, i * U7 + U7)
            dve.wait_ge(blank, 16)
            dve.wait_ge(loaded["neighbours"], 16 * 3)
            link(dve.tensor_scalar(rec[:, :, 1], srci, P - 1, None, ALU.bitwise_and))
            link(dve.tensor_copy(rec[:, :, 0], dsti))
            dve.wait_ge(prefix, 1)
            link(dve.tensor_scalar(nti[:, :], bank[7][:, 64:64 + W], float(GE - 1), None, ALU.add))
            link(dve.tensor_scalar(nti[:, :], nti[:, :], GE.bit_length() - 1, None, ALU.logical_shift_right))
            link(dve.tensor_scalar(ntf[:, :], nti[:, :], 1.0, None, ALU.max))
            link(dve.tensor_scalar(ntci[0:W, :], bank[7][0:W, 128:129], float(GE - 1), None, ALU.add))
            link(dve.tensor_scalar(ntci[0:W, :], ntci[0:W, :], GE.bit_length() - 1, None, ALU.logical_shift_right))
            dve.tensor_scalar(ntc[0:W, :], ntci[0:W, :], 1.0, None, ALU.max).then_inc(ntc_done, 1)
            dve.wait_ge(ntc_done, 1)
            link(dve.tensor_tensor_scan(tend[:, :], onesf[:, 0:W], ntf[:, :], 0.0, ALU.mult, ALU.add))
            link(dve.tensor_copy(tendi[:, 0:W], tend[:, :]))
            link(dve.memset(tendi[:, W:W + 1], 0))
            link(dve.tensor_tensor(ntf[:, :], tend[:, :], ntf[:, :], ALU.subtract))
            link(dve.scalar_tensor_tensor(base[:, :], ntf[:, :], float(GE), bank[7][:, 0:W], ALU.mult, ALU.add))
            link(dve.tensor_scalar(base[:, :], base[:, :], -1.0, None, ALU.add))
            dve.memset(started[:, 5:6], 0.0).then_inc(r_set, 1)
            for q, to in enumerate(CHUNKS):
                from_ = CHUNKS[q - 1] if q else 0
                cols = slice(from_, to)

                def mask(w, b):
                    dve.tensor_scalar(maskb[:, b, cols], winb[:, cols], iotap[:, ds(w, 1)], None, ALU.is_equal
                                      ).then_inc(r_mask, 1)

                with dve.Fori(0, W // U7) as i:
                    dve.wait_ge(r_set, i * U7 + (q * W + 1))
                    mask(i * U7, 0)
                    for u in range(U7):
                        w, b = i * U7 + u, u % 2
                        dve.wait_ge(r_mask, w + (q * W + 1))
                        dve.tensor_tensor_scan(rank[:, b, cols], onebf[:, cols], maskb[:, b, cols],
                                               base[:, ds(w, 1)], ALU.mult, ALU.add).then_inc(r_scan, 1)
                        dve.wait_ge(r_set, w + (q * W + 1))
                        if u + 1 < U7:
                            mask(w + 1, (u + 1) % 2)
                        dve.wait_ge(r_scan, w + (q * W + 1))
                        pause()
                        dve.tensor_copy(base[:, ds(w, 1)], rank[:, b, to - 1:to])
                        dve.copy_predicated(posf[:, cols], maskb[:, b, cols].bitcast(U16), rank[:, b, cols]
                                            ).then_inc(r_set, 1)
                dve.wait_ge(r_set, q * W + W + 1)
                link(dve.tensor_copy(slot[:, cols], posf[:, cols]))
                link(dve.tensor_scalar(srci[:, cols], slot[:, cols], P - 1, None, ALU.bitwise_and))
                link(dve.tensor_scalar(slot[:, cols], slot[:, cols], 7, None, ALU.logical_shift_right))
                dve.scalar_tensor_tensor(slot[:, cols], srci[:, cols], float(TP), slot[:, cols], ALU.mult, ALU.add
                                         ).then_inc(slot_done, 1)
            dve.wait_ge(prefix, 2)
            link(dve.tensor_copy(tsc[0:W, :], bank[6][0:W, 0:1]))
            link(dve.tensor_tensor(tec[0:W, :], tsc[0:W, :], ntc[0:W, :], ALU.add))
            dve.wait_ge(consts, 12)
            link(dve.tensor_scalar(stw[0:W, :], inw[0:W, :], tsc[0:W, :], None, ALU.is_ge))
            link(dve.scalar_tensor_tensor(stw[0:W, :], inw[0:W, :], tec[0:W, :], stw[0:W, :], ALU.is_lt, ALU.mult))
            link(dve.tensor_scalar(startw[0:W, :], inw[0:W, :], tsc[0:W, :], None, ALU.is_equal))
            link(dve.tensor_copy(inw[0:W, :], stw[0:W, :]))

            dve.wait_ge(loaded["x"], 32)
            with dve.Fori(0, W // U7) as i:
                for u in range(U7):
                    dve.bn_stats(stats7[:, u, :], xs[:, ds(i * U7 + u, 1), :].rearrange("p a c -> p (a c)")
                                 ).then_inc(stat1, 1)
                dve.wait_ge(stat1, i * U7 + U7)
                pause()
                for u in range(U7):
                    dve.bn_aggr(agg7[:, u, :], stats7[:, u, :]).then_inc(stat3, 1)
                dve.wait_ge(stat3, i * U7 + U7)
                pause()
                dve.tensor_copy(mv[:, ds(i * U7, U7), :], agg7[:, :, :]).then_inc(stat2, 1)
                dve.wait_ge(stat2, i + 1)
            dve.wait_ge(std_done, 1)
            dve.reciprocal(rs[:, :], sd[:, :]).then_inc(rstd_done, 1)
            dve.wait_ge(rstd_done, 1)
            link(dve.memset(tabh[:, :, D:D + 1], 1.0))
            link(dve.memset(tabh[:, :, D + 1:D + 2], 0.0))
            dve.wait_ge(loaded["weights"], 16 * 6)
            def normed(i):
                dve.tensor_scalar(xn[:, :], xs[:, ds(i, 1), :].rearrange("p a c -> p (a c)"), mv[:, ds(i, 1), 0],
                                  rs[:, ds(i, 1)], ALU.subtract, ALU.mult).then_inc(n_xn, 1)

            def node(i, more=True):
                dve.wait_ge(n_wh, i + 1)
                dve.tensor_tensor(wh[:, :], bank[1][:, 0:D], wbb[:, :], ALU.add).then_inc(n_tab, 1)
                if more:
                    dve.wait_ge(n_xt, i + 1)
                    normed(i + 1)
                dve.wait_ge(n_tab, i + 1)
                for n, a in enumerate((adst, asrc)):
                    dve.tensor_tensor(prod[:, n, :], wh[:, :], a[:, :], ALU.mult).then_inc(n_tab2, 1)
                dve.wait_ge(n_tab2, i * 2 + 1)
                dve.tensor_reduce(tab[:, ds(i, 1), D + 1], prod[:, 0, :], AX.X, ALU.add).then_inc(n_fd, 1)
                dve.wait_ge(n_kraw, i + 1)
                dve.scalar_tensor_tensor(kk[:, :], ek[:, :], 1.0, rk[:, :], ALU.min, ALU.add).then_inc(n_kk, 1)
                dve.wait_ge(n_qraw, i + 1)
                dve.scalar_tensor_tensor(qT[:, :, ds(i * P, P)], eq[:, :].rearrange("p (h n) -> p h n", h=2), 1.0,
                                         rq[:, :].rearrange("p (h n) -> p h n", h=2), ALU.min, ALU.add
                                         ).then_inc(n_qT, 1)
                dve.wait_ge(n_tab2, i * 2 + 2)
                dve.tensor_reduce(frc[:, ds(i, 1)], prod[:, 1, :], AX.X, ALU.add).then_inc(n_fd, 1)
                dve.wait_ge(n_hi, i + 1)
                dve.tensor_tensor(tabh[:, ds(i, 1), D + 2:2 * D + 2].rearrange("p a c -> p (a c)"), wh[:, :],
                                  tabh[:, ds(i, 1), 0:D].rearrange("p a c -> p (a c)"), ALU.subtract
                                  ).then_inc(n_lo, 1)
                dve.wait_ge(n_fd, i * 2 + 2)
                dve.wait_ge(n_lo, i + 1)

            normed(0)
            with dve.Fori(0, W - 1) as i:
                node(i)
            node(W - 1, False)

            dve.tensor_reduce(cmax[:, :], tab[:, :, D + 1], AX.X, ALU.max, apply_absolute_value=True
                              ).then_inc(c_in, 1)
            dve.wait_ge(c_ps, 1)
            dve.tensor_reduce(c1[:, :], bank[6][0:1, 0:P], AX.X, ALU.max).then_inc(c_in, 1)
            dve.wait_ge(c_ps, 2)
            link(dve.tensor_scalar(coff[:, :], bank[6][:, 0:1], 1.0, None, ALU.add))
            dve.wait_ge(c_ps, 3)
            dve.tensor_copy(frT[0:W, :], bank[7][0:W, 0:P]).then_inc(tiles_in, 1)
            link(dve.memset(bd[:, :, :], 0.0))
            dve.wait_ge(n_ctx, W)
            for hd in range(H):
                h, p = hd * DH // P, hd * DH % P
                dve.tensor_copy(bd[p:p + DH, h, hd * DH:(hd + 1) * DH], bank[4 + h][p:p + DH, hd * DH:(hd + 1) * DH])
                last = dve.tensor_copy(bd[p:p + DH, h, D + hd:D + hd + 1], bank[4 + h][p:p + DH, D:D + 1])
            last.then_inc(bd_done, 1)

            dve.wait_ge(table_out, 16)
            def attention(i):
                dve.wait_ge(a_num, i + 1)
                dve.tensor_scalar(dmx[:, :], bank[5][:, D:D + H], 1e-6, None, ALU.max).then_inc(a_dm, 1)
                dve.wait_ge(a_dm, i + 1)
                dve.reciprocal(dinv[:, :], dmx[:, :]).then_inc(a_di, 1)
                dve.wait_ge(a_di, i + 1)
                dve.tensor_tensor(att.rearrange("p (h d) -> p h d", h=H),
                                  bank[5][:, 0:D].rearrange("p (h d) -> p h d", h=H),
                                  dinv[:, :].rearrange("p (h a) -> p h a", a=1).to_broadcast([P, H, DH]), ALU.mult
                                  ).then_inc(a_att, 1)

            def add_projection(i):
                x_i = xs[:, ds(i, 1), :].rearrange("p a c -> p (a c)")
                dve.wait_ge(a_pj, i + 1)
                dve.tensor_tensor(mixs, bank[7][:, 0:D], bpb[:, :], ALU.add).then_inc(a_mix, 1)
                dve.wait_ge(a_mix, i + 1)
                dve.tensor_tensor(x_i, x_i, mixs, ALU.add).then_inc(a_x, 1)
                dve.wait_ge(a_x, i + 1)

            attention(0)
            with dve.Fori(0, W - 1) as i:
                attention(i + 1)
                add_projection(i)
            add_projection(W - 1)

            for n in range(2):
                dve.wait_ge(loaded["experts"], 16 * (n + 1))
                dve.wait_ge(w_hi, n + 1)
                dve.tensor_tensor(wparts[2 * n + 1], stagew_e, wparts[2 * n], ALU.subtract).then_inc(w_lo, 1)
            dve.wait_ge(loaded["experts"], 16 * 4)
            link(dve.memset(b2p, 0.0))
            link(dve.tensor_copy(b2p[0:1, :], stageb[0:1, :]))
            link(dve.tensor_copy(b2p[32:33, :], stageb[32:33, :]))
            link(dve.tensor_tensor(b2p[32:33, :], stageb[32:33, :], b2p[32:33, :], ALU.subtract))
            dve.memset(onesh, 1.0).then_inc(b_parts, 1)

            last_group = dve.alloc_register("last_group")
            window = dve.alloc_register("window")
            dve.reg_mov(window, 0)
            dve.reg_load(last_group, tendi[0:1, 0:1])
            link(dve.memset(U, 0.0))
            link(dve.memset(mx[:, GR - 1:GR], 0.0))
            link(dve.memset(pr[:, GR - 1, 1:2], 0.0))
            dve.wait_ge(meta_sb, 2)

            def one_hot(g, r, j):
                ins = dve.tensor_scalar(hot[:, r, j, :], iotab[:, :], m4[:, r, j:j + 1], None, ALU.is_equal)
                if j == GT - 1:
                    ins.then_inc(e_hot, 1)

            def largest(g, r):
                dve.wait_ge(e_VT, g + 1)
                dve.tensor_reduce(mloc[:, r:r + 1], bank[turned[r % 2]][:, :], AX.X, ALU.max).then_inc(e_ml, 1)

            def running(g, r):
                dve.wait_ge(e_ml, g + 1)
                dve.scalar_tensor_tensor(mx[:, r:r + 1], mx[:, (r - 1) % GR:(r - 1) % GR + 1],
                                         m4[:, r, GT:GT + 1], mloc[:, r:r + 1], ALU.mult, ALU.max
                                         ).then_inc(e_mx, 1)

            def top_score(g, r):
                dve.wait_ge(e_mx, g + 1)
                dve.scalar_tensor_tensor(cc[:, r:r + 1], mx[:, r:r + 1], coff[:, :], pr[:, r, 0:1],
                                         ALU.subtract, ALU.add).then_inc(e_cc, 1)

            def shift(g, r):
                dve.wait_ge(e_cc, g + 1)
                dve.scalar_tensor_tensor(pr[:, r, 1:2], cc[:, r:r + 1], ALPHA, cc[:, r:r + 1], ALU.mult, ALU.max
                                         ).then_inc(e_R, 1)

            def shift_change(g, r):
                dve.wait_ge(e_R, g + 1)
                dve.tensor_scalar(gc[:, r:r + 1], pr[:, (r - 1) % GR, 1:2], pr[:, r, 1:2], 0.0, ALU.subtract, ALU.min
                                  ).then_inc(e_gc, 1)

            def window_end(g):
                with dve.If(dve.snap(last_group) == g + 1):
                    w = dve.snap(window, min_val=0, max_val=W - 1)
                    dve.wait_ge(e_U, g + 1)
                    dve.tensor_scalar(dn[:, :], U[:, D:D + 1], 1e-30, None, ALU.max).then_inc(f_dn, 1)
                    dve.wait_ge(f_dn, w + 1)
                    dve.reciprocal(rd[:, :], dn[:, :]).then_inc(f_rd, 1)
                    dve.wait_ge(f_rd, w + 1)
                    dve.tensor_scalar(hh, U[:, 0:D], rd[:, :], 0.0, ALU.mult, ALU.max).then_inc(f_hh, 1)
                    dve.wait_ge(f_hh, w + 1)
                    x_w = xs[:, ds(w, 1), :].rearrange("p a c -> p (a c)")
                    dve.tensor_tensor(x_w, x_w, hh, ALU.add).then_inc(f_x, 1)
                    dve.wait_ge(f_x, w + 1)
                    pause()
                    dve.reg_load(last_group, tendi[0:1, ds(w + 1, 1)])
                    dve.reg_add(window, window, 1)

            def add_up(g, r, first=False):
                if not first:
                    dve.wait_ge(e_U, g)
                dve.wait_ge(e_gg, g + 1)
                dve.wait_ge(e_A, g + 1)
                dve.scalar_tensor_tensor(U, U, gg[:, r:r + 1], bank[2 + r % 2][:, 0:D + 1], ALU.mult, ALU.add
                                         ).then_inc(e_U, 1)

            def spread_of(r):
                return bank[spreads[r % 2]][:, 0:2 * GT].rearrange("p (j c) -> p j c", c=2)

            def edge_sum(g, r):
                dve.wait_ge(e_EX, g + 1)
                dve.tensor_tensor(s1[:, r, :], spread_of(r)[:, :, 0], G[:, r, :, D + 1], ALU.add).then_inc(e_s1, 1)

            def edge_score(g, r):
                dve.wait_ge(e_s1, g + 1)
                dve.scalar_tensor_tensor(s2[:, r, :], s1[:, r, :], ALPHA, s1[:, r, :], ALU.mult, ALU.max
                                         ).then_inc(e_s2, 1)

            def less_shift(g, r):
                dve.wait_ge(e_s2, g + 1)
                dve.tensor_tensor(s3[:, r, :], s2[:, r, :], spread_of(r)[:, :, 1], ALU.subtract).then_inc(e_s3, 1)

            def bounded(g, r):
                dve.wait_ge(e_s3, g + 1)
                dve.tensor_scalar(s4[:, r, :], s3[:, r, :], 0.0, None, ALU.min).then_inc(e_s4, 1)

            def second_part(g, r):
                dve.wait_ge(e_w4, g + 1)
                dve.tensor_tensor(w4l[:, r, :], w4[:, r, :], w4h[:, r, :], ALU.subtract).then_inc(e_w4l, 1)

            def weights(g, r, freed):
                dve.wait_ge(e_w4l, g + 1)
                if freed:
                    dve.wait_ge(e_A, g - 1)
                for j in range(GT):
                    ins = dve.tensor_scalar(Sp[1][:, r % 2, j, :], hot[:, r, j, :], w4l[:, r, j:j + 1], None,
                                            ALU.mult)
                ins.then_inc(e_Sl, 1)

            def step(g, r, first=False, left=NG):
                n, nr, s, sr, o, orr = g + 1, (r + 1) % GR, g + 2, (r + 2) % GR, g + 3, (r + 3) % GR
                scored = not (first and r < -1) and left > 1
                shifted = left > 2
                added = not (first and r < 1)
                if left > 3:
                    dve.wait_ge(e_m4, o + 1)
                    if not (first and r < 3):
                        dve.wait_ge(e_S, o - 5)
                        dve.wait_ge(e_Sl, o - 5)
                    for j in range(GT):
                        one_hot(o, orr, j)
                shift_steps = [largest, running, top_score, shift, shift_change] if shifted else []
                score_steps = [edge_sum, edge_score, less_shift, bounded] if scored else []
                for m in range(5):
                    if m < len(shift_steps):
                        shift_steps[m](s, sr)
                    if m < len(score_steps):
                        score_steps[m](n, nr)
                if added:
                    add_up(g - 1, (r - 1) % GR, first and r == 1)
                if scored:
                    second_part(n, nr)
                    weights(n, nr, added)
                if added:
                    window_end(g - 1)

            dve.wait_ge(e_m4, 1)
            for j in range(GT):
                one_hot(0, 0, j)
            for r in range(-2, GR):
                step(r, r, True)
            with dve.Fori(1, NGL) as i:
                for r in range(GR):
                    step(i * GR + r, r)
            for g in range(NGL * GR, NG):
                step(g, g % GR, left=NG - g)
            add_up(NG - 1, (NG - 1) % GR)
            window_end(NG - 1)

            with dve.Fori(0, W // U7) as i:
                for u in range(U7):
                    dve.bn_stats(stats7[:, u, :], xs[:, ds(i * U7 + u, 1), :].rearrange("p a c -> p (a c)")
                                 ).then_inc(m_st, 1)
                dve.wait_ge(m_st, i * U7 + U7)
                pause()
                for u in range(U7):
                    dve.bn_aggr(agg7[:, u, :], stats7[:, u, :]).then_inc(m_ag0, 1)
                dve.wait_ge(m_ag0, i * U7 + U7)
                pause()
                dve.tensor_copy(mv[:, ds(i * U7, U7), :], agg7[:, :, :]).then_inc(m_ag, 1)
                dve.wait_ge(m_ag, i + 1)
            dve.wait_ge(m_sd, 1)
            dve.reciprocal(rs[:, :], sd[:, :]).then_inc(m_rs, 1)
            dve.wait_ge(m_rs, 1)

            def norm(w, u):
                x_i = xs[:, ds(w, 1), :].rearrange("p a c -> p (a c)")
                dve.wait_ge(m_xt, w + (0 if u > 1 else 1))
                dve.wait_ge(m_x1, w + (0 if u > 1 else 1))
                dve.tensor_scalar(x2[u % 2], x_i, mv[:, ds(w, 1), 0], rs[:, ds(w, 1)], ALU.subtract, ALU.mult
                                  ).then_inc(m_x2, 1)

            def norm_lo(w, u):
                cols = ds(w * P, P)
                dve.wait_ge(m_xhi, w + 2)
                dve.tensor_tensor(x2p[1][:, :, cols], x2T[u % 3], x2p[0][:, :, cols], ALU.subtract
                                  ).then_inc(m_xlo, 1)

            def norm_add(w, u):
                x_i = xs[:, ds(w, 1), :].rearrange("p a c -> p (a c)")
                dve.wait_ge(m_x2, w + 1)
                dve.tensor_tensor(x_i, x_i, x2[u % 2], ALU.add).then_inc(m_x1, 1)

            for n, m in enumerate((m_xt, m_x1, m_xlo, m_lg, m_xhi)):
                dve.memset(none[:, n:n + 1], 0.0).then_inc(m, 1)
            with dve.Fori(0, W // U7) as i:
                for u in range(U7 + 2):
                    w = i * U7 + u
                    if u < U7:
                        norm(w, u)
                    if u > 1:
                        norm_lo(w - 2, u - 2)
                    if u < U7:
                        norm_add(w, u)
            dve.memset(started[:, 1:2], 0.0).then_inc(m_lo, 1)
            dve.memset(started[:, 2:3], 0.0).then_inc(m_gelu, 4)
            dve.memset(started[:, 3:4], 0.0).then_inc(m_y, 2 * NB)
            dve.memset(started[:, 4:5], 0.0).then_inc(m_acc, NB)

            def wide(a):
                return a[:, :].rearrange("p (w a) -> p w a", a=1).to_broadcast([P, W, X])

            keys = from_end[:, :].rearrange("p (a e) -> p a e", a=1).to_broadcast([P, W, X])
            dve.wait_ge(m_lg, W + 1)
            link(dve.tensor_copy(lg, bank[1][:, 0:W * X].rearrange("p (w e) -> p w e", e=X)))
            link(dve.tensor_reduce(top[:, :], lg, AX.X, ALU.max))
            dve.tensor_tensor(lg, lg, wide(top), ALU.subtract).then_inc(m_diff, 1)
            dve.wait_ge(m_diff, 1)

            def largest_of(v, one, value):
                link(dve.tensor_tensor(one, v, value, ALU.is_equal))
                link(dve.tensor_tensor(one, one, keys, ALU.mult))
                link(dve.tensor_reduce(key[:, :], one, AX.X, ALU.max))
                link(dve.tensor_tensor(one, keys, wide(key), ALU.is_equal))

            link(dve.memset(top[:, :], 0.0))
            largest_of(lg, one1, wide(top))
            link(dve.scalar_tensor_tensor(sc, one1, -3e38, lg, ALU.mult, ALU.add))
            link(dve.tensor_reduce(top[:, :], sc, AX.X, ALU.max))
            largest_of(sc, one2, wide(top))
            link(dve.tensor_tensor(one1, one1, one2, ALU.add))
            def split(k, b, n):
                dve.wait_ge(m_hi, k + 1)
                dve.tensor_tensor(hTp[1][:, b, :, 0:n * P], hT[:, :, 0:n * P], hTp[0][:, b, :, 0:n * P],
                                  ALU.subtract).then_inc(m_lo, 1)

            split(0, 0, NB)
            dve.wait_ge(m_ex, 1)
            link(dve.tensor_reduce(tot[:, :], ex, AX.X, ALU.add))
            link(dve.reciprocal(rt[:, :], tot[:, :]))
            link(dve.tensor_tensor(ex, ex, wide(rt), ALU.mult))
            link(dve.tensor_tensor(sc, ex, one1, ALU.mult))
            link(dve.tensor_reduce(tot[:, :], sc, AX.X, ALU.add))
            link(dve.tensor_scalar(tot[:, :], tot[:, :], 1e-12, None, ALU.max))
            link(dve.reciprocal(rt[:, :], tot[:, :]))
            link(dve.tensor_tensor(comb, sc, wide(rt), ALU.mult))

            def add(y, i, e, n):
                for j in range(n):
                    dve.wait_ge(m_y, y + (2 * NB + j + 1))
                    dve.wait_ge(m_acc, y + (NB - (n if e else NB) + j + 1))
                    x_w = xs[:, ds(i * NB + j, 1), :].rearrange("p a c -> p (a c)")
                    dve.scalar_tensor_tensor(x_w, bank[j][:, 0:D], comb[:, ds(i * NB + j, 1), e], x_w,
                                             ALU.mult, ALU.add).then_inc(m_acc, 1)

            def batch(i, n, after):
                for e in range(X):
                    if e + 1 < X:
                        split(i * X + (e + 1), (e + 1) % 2, n)
                    elif after:
                        split(i * X + (e + 1), (e + 1) % 2, after)
                    add(i * (NB * X) + n * e, i, e, n)

            dve.wait_ge(m_x1, W + 1)
            with dve.Fori(0, FULL - 1) as i:
                batch(i, NB, NB)
            batch(FULL - 1, NB, REST)
            batch(FULL, REST, 0)


_INS = ['x', 'src', 'dst', 'L0_gnn_W_w', 'L0_gnn_W_b', 'L0_gnn_a_w', 'L0_gnn_a_b', 'L0_mix_Wq', 'L0_mix_Wkv',
        'L0_mix_Wproj', 'L0_mix_bproj', 'L0_ffn_router_w', 'L0_ffn_w1', 'L0_ffn_b1', 'L0_ffn_w2', 'L0_ffn_b2']


def kernel(**inputs):
    import numpy as _np
    import concourse.bacc as _bacc
    from concourse import mybir as _mybir
    from concourse.bass_utils import run_bass_kernel_spmd as _run

    nc = _bacc.Bacc("TRN2", target_bir_lowering=False, num_devices=1)
    arrays, args = {}, []
    for name in _INS:
        a = _np.ascontiguousarray(inputs[name])
        arrays[f"in_{name}_dram"] = a
        args.append(nc.dram_tensor(f"in_{name}_dram", a.shape, _mybir.dt.from_np(a.dtype), kind="ExternalInput").ap())
    shape = inputs['x'].shape
    args.append(nc.dram_tensor("out_dram", shape, _mybir.dt.float32, kind="ExternalOutput").ap())
    graph_layer(nc, *args)
    return _run(nc, [arrays], core_ids=[0]).results[0]["out_dram"]
```
